# Optimizing a Trainium2 kernel written in Bass

```python
import numpy as np
import jax
import jax.numpy as jnp

def _softmax(x, axis=-1):
    return jax.nn.softmax(x, axis=axis)
def _gelu(x):
    return jax.nn.gelu(x, approximate=True)
def _silu(x):
    return jax.nn.silu(x)
def _sigmoid(x):
    return jax.nn.sigmoid(x)
def _layernorm(x, axis=-1, eps=1e-5):
    m = jnp.mean(x, axis=axis, keepdims=True)
    v = jnp.var(x, axis=axis, keepdims=True)
    return (x - m) / jnp.sqrt(v + eps)
def _scatter_add(tgt, idx, src, axis=0):
    return tgt.at[idx].add(src)
def _segment_sum(src, seg, n):
    return jax.ops.segment_sum(src, seg, n)

kernel_name = 'mk_conv_seq_d2_conv_nchw64_fa0c7b'

def setup_inputs(seed: int = 0):
    np.random.seed(seed)
    _w = jnp.asarray
    def _rec_inputs():
        import jax
        import jax.numpy as jnp
        _gk = jax.random.key(seed)
        x = -0.000125 + 0.9999 * jax.random.normal(jax.random.fold_in(_gk, 1), (8, 64, 256, 256), jnp.float32)
        return x
    x = _rec_inputs()
    def _L0_conv_setup():
        import jax, jax.numpy as jnp
        import numpy as np
        WS = 8
        NH = 4
        DIM = 64
        HID = 256
        EPS = 1e-05

        def _rel_pos_index(ws):
            coords = np.stack(np.meshgrid(np.arange(ws), np.arange(ws), indexing='ij')).reshape(2, -1)
            rel = (coords[:, :, None] - coords[:, None, :]).transpose(1, 2, 0)
            rel[..., 0] += ws - 1
            rel[..., 1] += ws - 1
            rel[..., 0] *= 2 * ws - 1
            return rel.sum(-1)

        def _layernorm(x, g, b):
            mu = x.mean(-1, keepdims=True)
            var = ((x - mu) ** 2).mean(-1, keepdims=True)
            return (x - mu) * jax.lax.rsqrt(var + EPS) * g + b
        key = jax.random.key(seed)
        ks = jax.random.split(key, 16)
        s = 0.02
        return {'x': jax.random.normal(ks[0], (8, DIM, 256, 256), jnp.float32), 'qkv_w': jax.random.normal(ks[1], (DIM, 3 * DIM), jnp.float32) * s, 'qkv_b': jnp.zeros((3 * DIM,), jnp.float32), 'proj_w': jax.random.normal(ks[2], (DIM, DIM), jnp.float32) * s, 'proj_b': jnp.zeros((DIM,), jnp.float32), 'rpb_table': jax.random.normal(ks[3], ((2 * WS - 1) ** 2, NH), jnp.float32) * s, 'norm1_g': jnp.ones((DIM,), jnp.float32), 'norm1_b': jnp.zeros((DIM,), jnp.float32), 'norm2_g': jnp.ones((DIM,), jnp.float32), 'norm2_b': jnp.zeros((DIM,), jnp.float32), 'ffn_w1': jax.random.normal(ks[4], (DIM, HID), jnp.float32) * s, 'ffn_b1': jnp.zeros((HID,), jnp.float32), 'ffn_w2': jax.random.normal(ks[5], (HID, DIM), jnp.float32) * s, 'ffn_w2_b': jnp.zeros((DIM,), jnp.float32), 'dw_w': jax.random.normal(ks[6], (DIM, 1, 3, 3), jnp.float32) * s, 'dw_b': jnp.zeros((DIM,), jnp.float32)}
    _L0_conv_all = _L0_conv_setup()
    _L0_conv_in = {k: v for k, v in _L0_conv_all.items() if k in ('qkv_w', 'qkv_b', 'proj_w', 'proj_b', 'rpb_table', 'norm1_g', 'norm1_b', 'norm2_g', 'norm2_b', 'ffn_w1', 'ffn_b1', 'ffn_w2', 'ffn_w2_b', 'dw_w', 'dw_b', )}
    del _L0_conv_all

    def _L1_conv_setup():
        import jax, jax.numpy as jnp
        import numpy as np
        K = 3
        D = 1
        G = 8
        BN_EPS = 1e-05
        key = jax.random.key(seed)
        ks = jax.random.split(key, 8)
        N, C, H, W = (8, 64, 256, 256)
        k2 = K * K
        x = jax.random.normal(ks[0], (N, C, H, W), jnp.float32)
        conv_w = jax.random.normal(ks[1], (G * k2, C), jnp.float32) * (2.0 / C) ** 0.5
        bn_gamma = jnp.ones((G * k2,), jnp.float32)
        bn_beta = jnp.zeros((G * k2,), jnp.float32)
        bn_mean = jax.random.normal(ks[2], (G * k2,), jnp.float32) * 0.01
        bn_var = jax.random.uniform(ks[3], (G * k2,), jnp.float32, 0.5, 1.5)
        lamb_l = jax.random.normal(ks[4], (C,), jnp.float32) * 0.1
        lamb_h = jax.random.normal(ks[5], (C,), jnp.float32) * 0.1
        inside_all = jax.random.normal(ks[6], (C, 1, 1), jnp.float32) * 0.1
        return {'x': x, 'conv_w': conv_w, 'bn_gamma': bn_gamma, 'bn_beta': bn_beta, 'bn_mean': bn_mean, 'bn_var': bn_var, 'lamb_l': lamb_l, 'lamb_h': lamb_h, 'inside_all': inside_all}
    _L1_conv_all = _L1_conv_setup()
    _L1_conv_in = {k: v for k, v in _L1_conv_all.items() if k in ('conv_w', 'bn_gamma', 'bn_beta', 'bn_mean', 'bn_var', 'lamb_l', 'lamb_h', 'inside_all', )}
    del _L1_conv_all

    return {
        "x": x,
        "L0_conv_qkv_w": _L0_conv_in["qkv_w"],
        "L0_conv_qkv_b": _L0_conv_in["qkv_b"],
        "L0_conv_proj_w": _L0_conv_in["proj_w"],
        "L0_conv_proj_b": _L0_conv_in["proj_b"],
        "L0_conv_rpb_table": _L0_conv_in["rpb_table"],
        "L0_conv_norm1_g": _L0_conv_in["norm1_g"],
        "L0_conv_norm1_b": _L0_conv_in["norm1_b"],
        "L0_conv_norm2_g": _L0_conv_in["norm2_g"],
        "L0_conv_norm2_b": _L0_conv_in["norm2_b"],
        "L0_conv_ffn_w1": _L0_conv_in["ffn_w1"],
        "L0_conv_ffn_b1": _L0_conv_in["ffn_b1"],
        "L0_conv_ffn_w2": _L0_conv_in["ffn_w2"],
        "L0_conv_ffn_w2_b": _L0_conv_in["ffn_w2_b"],
        "L0_conv_dw_w": _L0_conv_in["dw_w"],
        "L0_conv_dw_b": _L0_conv_in["dw_b"],
        "L1_conv_conv_w": _L1_conv_in["conv_w"],
        "L1_conv_bn_gamma": _L1_conv_in["bn_gamma"],
        "L1_conv_bn_beta": _L1_conv_in["bn_beta"],
        "L1_conv_bn_mean": _L1_conv_in["bn_mean"],
        "L1_conv_bn_var": _L1_conv_in["bn_var"],
        "L1_conv_lamb_l": _L1_conv_in["lamb_l"],
        "L1_conv_lamb_h": _L1_conv_in["lamb_h"],
        "L1_conv_inside_all": _L1_conv_in["inside_all"],
    }

def reference(x, L0_conv_qkv_w, L0_conv_qkv_b, L0_conv_proj_w, L0_conv_proj_b, L0_conv_rpb_table, L0_conv_norm1_g, L0_conv_norm1_b, L0_conv_norm2_g, L0_conv_norm2_b, L0_conv_ffn_w1, L0_conv_ffn_b1, L0_conv_ffn_w2, L0_conv_ffn_w2_b, L0_conv_dw_w, L0_conv_dw_b, L1_conv_conv_w, L1_conv_bn_gamma, L1_conv_bn_beta, L1_conv_bn_mean, L1_conv_bn_var, L1_conv_lamb_l, L1_conv_lamb_h, L1_conv_inside_all):
    import jax
    import jax.numpy as jnp
    def _L0_conv_ref(x, qkv_w, qkv_b, proj_w, proj_b, rpb_table, norm1_g, norm1_b, norm2_g, norm2_b, ffn_w1, ffn_b1, ffn_w2, ffn_w2_b, dw_w, dw_b):
        import jax, jax.numpy as jnp
        import numpy as np
        WS = 8
        NH = 4
        DIM = 64
        HID = 256
        EPS = 1e-05

        def _rel_pos_index(ws):
            coords = np.stack(np.meshgrid(np.arange(ws), np.arange(ws), indexing='ij')).reshape(2, -1)
            rel = (coords[:, :, None] - coords[:, None, :]).transpose(1, 2, 0)
            rel[..., 0] += ws - 1
            rel[..., 1] += ws - 1
            rel[..., 0] *= 2 * ws - 1
            return rel.sum(-1)

        def _layernorm(x, g, b):
            mu = x.mean(-1, keepdims=True)
            var = ((x - mu) ** 2).mean(-1, keepdims=True)
            return (x - mu) * jax.lax.rsqrt(var + EPS) * g + b
        B, C, H, W = x.shape
        ws, nh = (WS, NH)
        hd = C // nh
        N = ws * ws
        assert H % ws == 0 and W % ws == 0
        x_hw = jnp.transpose(x, (0, 2, 3, 1))
        xn = _layernorm(x_hw, norm1_g, norm1_b)
        win = xn.reshape(B, H // ws, ws, W // ws, ws, C).transpose(0, 1, 3, 2, 4, 5)
        win = win.reshape(-1, N, C)
        qkv = win @ qkv_w + qkv_b
        qkv = qkv.reshape(-1, N, 3, nh, hd).transpose(2, 0, 3, 1, 4)
        q, k, v = (qkv[0], qkv[1], qkv[2])
        scale = hd ** (-0.5)
        attn = jnp.einsum('bhnd,bhmd->bhnm', q, k) * scale
        idx = _rel_pos_index(ws)
        bias = rpb_table[idx.reshape(-1)].reshape(N, N, nh).transpose(2, 0, 1)
        attn = jax.nn.softmax(attn + bias[None], axis=-1)
        out = jnp.einsum('bhnm,bhmd->bhnd', attn, v)
        out = out.transpose(0, 2, 1, 3).reshape(-1, N, C)
        out = out @ proj_w + proj_b
        out = out.reshape(B, H // ws, W // ws, ws, ws, C).transpose(0, 1, 3, 2, 4, 5)
        out = out.reshape(B, H, W, C)
        x_hw = x_hw + out
        xn = _layernorm(x_hw, norm2_g, norm2_b)
        ffn = jax.nn.gelu(xn @ ffn_w1 + ffn_b1, approximate=False) @ ffn_w2 + ffn_w2_b
        xc = jnp.transpose(x_hw, (0, 3, 1, 2))
        xc = jax.lax.conv_general_dilated(xc, dw_w, window_strides=(1, 1), padding=((1, 1), (1, 1)), feature_group_count=C, dimension_numbers=('NCHW', 'OIHW', 'NCHW')) + dw_b[None, :, None, None]
        xc = jnp.transpose(xc, (0, 2, 3, 1))
        x_hw = x_hw + ffn + xc
        return jnp.transpose(x_hw, (0, 3, 1, 2))

    def _L1_conv_ref(x, conv_w, bn_gamma, bn_beta, bn_mean, bn_var, lamb_l, lamb_h, inside_all):
        import jax, jax.numpy as jnp
        import numpy as np
        K = 3
        D = 1
        G = 8
        BN_EPS = 1e-05
        N, C, H, W = x.shape
        k2 = K * K
        pooled = x.mean(axis=(2, 3))
        lf = pooled @ conv_w.T
        lf = (lf - bn_mean) * (bn_gamma / jnp.sqrt(bn_var + BN_EPS)) + bn_beta
        lf = jnp.tanh(lf).reshape(N, G, 1, k2, 1)
        p = D * (K - 1) // 2
        xp = jnp.pad(x, ((0, 0), (0, 0), (p, p), (p, p)), mode='reflect')
        patches = jnp.stack([xp[:, :, i * D:i * D + H, j * D:j * D + W] for i in range(K) for j in range(K)], axis=2)
        xu = patches.reshape(N, G, C // G, k2, H * W)
        low_part = jnp.sum(xu * lf, axis=3).reshape(N, C, H, W)
        gap = x.mean(axis=(2, 3), keepdims=True)
        out_low = (low_part * (inside_all + 1.0) - inside_all * gap) * lamb_l[None, :, None, None]
        out_high = x * (lamb_h[None, :, None, None] + 1.0)
        return out_low + out_high

    def _gn(v, G=32, eps=1e-5):
        B_, C_, H_, W_ = v.shape
        g = v.reshape(B_, G, C_ // G, H_, W_)
        m = jnp.mean(g, axis=(2, 3, 4), keepdims=True)
        s = jnp.var(g, axis=(2, 3, 4), keepdims=True)
        return ((g - m) / jnp.sqrt(s + eps)).reshape(v.shape)

    def _ln_c(v, eps=1e-6):
        m = jnp.mean(v, axis=1, keepdims=True)
        s = jnp.var(v, axis=1, keepdims=True)
        return (v - m) / jnp.sqrt(s + eps)

    def _ln_t(v, eps=1e-5):
        m = jnp.mean(v, axis=-1, keepdims=True)
        s = jnp.var(v, axis=-1, keepdims=True)
        return (v - m) / jnp.sqrt(s + eps)

    def _to_tokens(v):
        B_, C_, H_, W_ = v.shape
        return v.reshape(B_, C_, H_ * W_).transpose(0, 2, 1)
    def _from_tokens(t, like):
        B_, C_, H_, W_ = like.shape
        return t.transpose(0, 2, 1).reshape(B_, C_, H_, W_)

    x = _L0_conv_ref(x, L0_conv_qkv_w, L0_conv_qkv_b, L0_conv_proj_w, L0_conv_proj_b, L0_conv_rpb_table, L0_conv_norm1_g, L0_conv_norm1_b, L0_conv_norm2_g, L0_conv_norm2_b, L0_conv_ffn_w1, L0_conv_ffn_b1, L0_conv_ffn_w2, L0_conv_ffn_w2_b, L0_conv_dw_w, L0_conv_dw_b)
    x = _L1_conv_ref(x, L1_conv_conv_w, L1_conv_bn_gamma, L1_conv_bn_beta, L1_conv_bn_mean, L1_conv_bn_var, L1_conv_lamb_l, L1_conv_lamb_h, L1_conv_inside_all)
    return x


_drawn_inputs = setup_inputs


def setup_inputs(seed=0):
    import zlib

    import numpy as np

    out = dict(_drawn_inputs(seed))
    spreads = {'L0_conv_qkv_b': (0.0, 0.467),
     'L0_conv_proj_b': (0.0, 0.1),
     'L0_conv_norm1_g': (1.0, 0.6),
     'L0_conv_norm1_b': (0.0, 0.8),
     'L0_conv_norm2_g': (1.0, 0.6),
     'L0_conv_norm2_b': (0.0, 2.0),
     'L0_conv_ffn_b1': (0.0, 0.399),
     'L0_conv_ffn_w2_b': (0.0, 0.1),
     'L0_conv_dw_b': (0.0, 0.1),
     'L1_conv_bn_gamma': (1.0, 0.6),
     'L1_conv_bn_beta': (0.0, 0.309)}
    factors = {'L0_conv_qkv_w': 8.0,
     'L0_conv_proj_w': 3.399,
     'L0_conv_rpb_table': 8.0,
     'L1_conv_bn_mean': 38.124,
     'L1_conv_bn_var': 26.184,
     'L1_conv_inside_all': 5.953}
    for name, (base, spread) in spreads.items():
        noise = np.random.default_rng([zlib.crc32(name.encode()), seed]).standard_normal(out[name].shape)
        drawn = base * np.exp(spread * noise) if base else spread * noise
        out[name] = jnp.asarray(drawn.astype(out[name].dtype))
    for name, factor in factors.items():
        out[name] = (out[name] * factor).astype(out[name].dtype)
    return out
```

```python
from contextlib import ExitStack

import concourse.bass as bass
from concourse import mybir

F32 = mybir.dt.float32
BF16 = mybir.dt.bfloat16
ALU = mybir.AluOpType
ACT = mybir.ActivationFunctionType
AX = mybir.AxisListType

C = 64
WS = 8
NH = 4
HD = C // NH
HID = 256
IMG = 256
B = 8
PAIRS = B // 2
TILES = IMG // WS
TOK = WS * IMG
NW = IMG // WS
BANK = 512
NCH = TOK // BANK
ROUNDS = NW // 2
LN_EPS = 1e-5
BN_EPS = 1e-5
G = 8
K2 = 9
YROWS = 10 + IMG
Y0 = 9
HC = HID // 128
FLUSH_STEPS = 7 + 2 + 7 + 2 + 2 + 3 + 3


def halves():
    return ((0, slice(0, 64)), (1, slice(64, 128)))


def bass_window_block(nc, a, out):
    with ExitStack() as ctx:
        def sb(name, shape, dt=F32):
            return ctx.enter_context(nc.sbuf_tensor(name, shape, dt))

        def sem(name):
            return ctx.enter_context(nc.semaphore(name))

        ident = sb("ident", [128, 128])
        ident_bf = sb("ident_bf", [128, 128], BF16)
        centre = sb("centre", [128, 128])
        mean_of = sb("mean_of", [128, 2])
        headmask = sb("headmask", [128, NH])
        gsel = sb("gsel", [G * K2, C])
        kmask = sb("kmask", [G * K2, K2])
        pick_row = sb("pick_row", [32, 16, 128])
        pick_max = sb("pick_max", [128, NCH, 2, 8, 128], BF16)
        w_u = sb("w_u", [128, NH, 128])
        b_u = sb("b_u", [128, NH])
        w_v = sb("w_v", [128, C])
        w_p = sb("w_p", [128, 2, 2, 128])
        b_p = sb("b_p", [128, 1])
        w_1 = sb("w_1", [128, HID])
        b_1 = sb("b_1", [128, HC])
        w_2 = sb("w_2", [128, HC, C])
        b_y = sb("b_y", [128, 1])
        taps0 = sb("taps0", [128, K2])
        bias_t = sb("bias_t", [128, NH, 64])
        bias_part = [sb(f"bias_part{j}", [128, NH, 64], BF16) for j in range(3)]
        bias_g = sb("bias_g", [128, 2, 64], BF16)
        cols = sb("cols", [128, 16])
        raw_w = sb("raw_w", [128, 3 * C])
        raw_p = sb("raw_p", [128, C])
        raw_1 = sb("raw_1", [128, HID])
        gain_w = sb("gain_w", [128, 3 * C])
        gain_1 = sb("gain_1", [128, HID])
        qk_t = sb("qk_t", [128, 2 * C])
        q_masked = sb("q_masked", [128, NH, C])
        vecs = sb("vecs", [128, 12])
        conv_w_t = sb("conv_w_t", [128, G * K2])
        bn = sb("bn", [G * K2, 8])
        lf = sb("lf", [G * K2, 2])
        lf_k = sb("lf_k", [G * K2, 2, K2])
        taps1 = sb("taps1", [128, K2])
        l1c = sb("l1c", [128, 8])
        const1 = sb("const1", [128, 1])
        half_neg = sb("half_neg", [128, 32])

        x_in = sb("x_in", [128, TOK])
        xb = sb("xb", [128, TOK])
        sq = sb("sq", [128, TOK])
        z1 = sb("z1", [128, NW, 64])
        u = sb("u", [128, NW, NH, 64])
        v = sb("v", [128, NW, 2, 33])
        var = sb("var", [128, 32])
        rstd = sb("rstd", [128, 32])
        rstd_t = sb("rstd_t", [32, 128])
        mx = sb("mx", [128, 128], BF16)
        mx_t = sb("mx_t", [128, 128], BF16)
        prob = sb("prob", [128, 4, BANK])
        rsum = sb("rsum", [128, 2, 8])
        o_n = sb("o_n", [128, 2, 128])
        o_t = sb("o_t", [128, 4, 128])
        x1 = sb("x1", [128, WS + 2, IMG + 2])
        z2 = sb("z2", [128, TOK])
        hid = sb("hid", [128, 2, 4, BANK])
        f = sb("f", [128, WS + 1, IMG])
        y = sb("y", [128, WS, IMG])
        acc = sb("acc", [128, 2])
        tot = sb("tot", [128, 1])
        mean2 = sb("mean2", [128, 2])
        flags = sb("flags", [128, 2])
        y_in = u[:, :, :, :].rearrange("p a b c -> p (a b c)")[:, 0:2 * 10 * 258].rearrange(
            "p (n r w) -> p n r w", n=2, r=10)
        res = hid[:, :, :, :].rearrange("p n j t -> p n (j t)").rearrange("p n (r w) -> p n r w", w=IMG)

        ps = ctx.enter_context(nc.psum_tensor("ps", [128, 8, BANK], F32))
        wide = ps[:, 0:4, :]
        s_bank, o_bank, m_bank = 4, 6, 7
        turned_bank = (3, 3, 3, 0)

        y_dram = nc.dram_tensor("y_scratch", [B, C, YROWS, IMG], F32, kind="Internal").ap()

        names = """const_loaded prep_mm prep_ev dve_chain dve_prep bn_root bn_var flush_chain pool_prep ready x_loaded centred squared stats var_ready rstd_ready
            rstd_tp rstd_copied spread z_ready u_mm u_ready guard_mm guard_max v_mm v_ready max_tp max_copied
            score_mm exp_done pv_mm o_recip o_ready o_tp o_copied proj_mm xb_ready x1_ready f1_mm gelu_done f2_mm f_ready
            conv_step conv_done y_done carried y_stored flush_step flush_done phase2_ready lf_mm lf_act lf_dve edge_done y_loaded0 y_loaded1
            tap_first0 tap_first1 tap_step0 tap_step1 res_done0 res_done1 out_stored0 out_stored1 tot_step phase2_done row_fix z_init""".split()
        S = {n: sem(n) for n in names}

        xv = a["x"].rearrange("b c (i h) w -> b i c (h w)", h=WS)
        ctx.enter_context(nc.allow_non_contiguous_dma(reason="small weights"))
        block = ctx.enter_context(nc.Block())

        QB, PB, G1, B1N, G2, B2N, FB, DB, VB, KB = range(10)

        n_const = [0]

        @block.sync
        def _(sp):
            def ld(dst, src):
                sp.dma_start(dst, src).then_inc(S["const_loaded"], 16)
                n_const[0] += 16

            ld(ident[:], a["c_ident"])
            ld(centre[:], a["c_centre"])
            ld(mean_of[:], a["c_mean"])
            ld(headmask[:], a["c_head"])
            ld(gsel[:], a["c_gsel"])
            ld(kmask[:], a["c_kmask"])
            qkv_b = a["qkv_b"].rearrange("(k c o) -> k c o", k=3, o=1)

            def column(name):
                return a[name].rearrange("(c o) -> c o", o=1)

            for s, h in halves():
                ld(raw_w[h, :], a["qkv_w"])
                ld(raw_p[h, :], a["proj_w"])
                ld(raw_1[h, :], a["ffn_w1"])
                for k, src in ((QB, qkv_b[0]), (KB, qkv_b[1]), (VB, qkv_b[2]), (PB, column("proj_b")),
                               (G1, column("norm1_g")), (B1N, column("norm1_b")), (G2, column("norm2_g")),
                               (B2N, column("norm2_b")), (FB, column("ffn_w2_b")), (DB, column("dw_b"))):
                    ld(cols[h, k:k + 1], src)
                ld(taps0[h, :], a["dw_w"].rearrange("c o i j -> c (o i j)"))
                ld(l1c[h, 0:1], column("lamb_l"))
                ld(l1c[h, 1:2], column("lamb_h"))
                ld(l1c[h, 2:3], a["inside_all"].rearrange("c a b -> c (a b)"))
                ld(conv_w_t[h, :], a["conv_w"].rearrange("g c -> c g"))
            ld(b_1[:], a["ffn_b1"].rearrange("(k p) -> p k", k=HC))
            ld(w_2[:], a["ffn_w2"].rearrange("(k p) c -> p k c", k=HC))
            for k, name in enumerate(("bn_gamma", "bn_beta", "bn_mean", "bn_var")):
                ld(bn[:, k:k + 1], column(name))
            tab = a["rpb_t"]
            for m in range(64):
                r0, c0 = WS - 1 - m // WS, WS - 1 - m % WS
                for s in range(2):
                    src = tab.rearrange("h (r c) -> h r c", c=2 * WS - 1)[:, r0:r0 + WS, c0:c0 + WS]
                    ld(bias_t[64 * s + m:64 * s + m + 1, :, :].rearrange("p h (r c) -> p h r c", c=WS),
                       src.rearrange("(o h) r c -> o h r c", o=1))
            sp.wait_ge(S["z_init"], 1)
            for w in range(2):
                for h2 in range(2):
                    for s in range(2):
                        for hp in range(2):
                            p0 = 64 * s + 32 * w + 16 * hp
                            ld(w_p[p0:p0 + 16, w, h2, 64 * s:64 * s + 64],
                               a["proj_w"][HD * (2 * hp + h2):HD * (2 * hp + h2 + 1), :])

            def load_x(p, i):
                for s, h in halves():
                    sp.dma_start(x_in[h, :], xv[p + PAIRS * s, i, :, :]).then_inc(S["x_loaded"], 16)

            def next_x(T, p, i):
                sp.wait_ge(S["xb_ready"], T + 1)
                sp.wait_ge(S["z_ready"], 2 * T + 1)
                load_x(p, i)

            def phase2(p):
                sp.wait_ge(S["y_stored"], (p + 1) * 32 * (TILES + 2))
                for s in range(2):
                    yb = y_dram[p + PAIRS * s, :, :, :]
                    sp.dma_start(yb[:, Y0 - 1, :], yb[:, Y0 + 1, :]).then_inc(S["row_fix"], 16)
                    sp.dma_start(yb[:, Y0 + IMG, :], yb[:, Y0 + IMG - 2, :]).then_inc(S["row_fix"], 16)
                sp.wait_ge(S["row_fix"], (p + 1) * 64)

                def load_y(n, i):
                    for s, h in halves():
                        sp.dma_start(y_in[h, n, :, 1:257],
                                     y_dram[p + PAIRS * s, :, bass.ds(i * WS + Y0 - 1, WS + 2), :]
                                     ).then_inc(S[f"y_loaded{n}"], 16)

                sp.wait_ge(S["phase2_ready"], p + 1)
                load_y(0, 0)
                load_y(1, 1)
                with sp.Fori(0, TILES // 2 - 1) as j:
                    N = p * (TILES // 2) + j
                    for n in range(2):
                        sp.wait_ge(S[f"res_done{n}"], N + 1)
                        load_y(n, 2 * j + 2 + n)

            load_x(0, 0)
            with sp.Fori(0, PAIRS - 1) as p:
                with sp.Fori(0, TILES - 1) as i:
                    next_x(p * TILES + i, p, i + 1)
                next_x(p * TILES + TILES - 1, p + 1, 0)
                phase2(p)
            with sp.Fori(0, TILES - 1) as i:
                next_x((PAIRS - 1) * TILES + i, PAIRS - 1, i + 1)
            phase2(PAIRS - 1)

        @block.gpsimd
        def _(pool):
            nc.gpsimd.memset(half_neg[:], -0.5).then_inc(S["pool_prep"], 1)
            pool.wait_ge(S["pool_prep"], 1)
            pool.wait_ge(S["bn_var"], 1)
            nc.gpsimd.tensor_tensor(bn[:, 7:8], bn[:, 6:7], half_neg[0:G * K2, 0:1], ALU.pow).then_inc(S["bn_root"], 1)
            pool.wait_ge(S["ready"], 1)
            with pool.Fori(0, PAIRS) as p:
                with pool.Fori(0, TILES) as i:
                    T = p * TILES + i
                    pool.wait_ge(S["x_loaded"], 32 * T + 32)
                    pool.wait_ge(S["x1_ready"], 4 * T + 1)
                    nc.gpsimd.tensor_tensor(xb[:], x_in[:], b_p[:, 0:1].broadcast_to([128, TOK]),
                                            ALU.add).then_inc(S["xb_ready"], 1)
                    for k in range(2):
                        pool.wait_ge(S["var_ready"], 2 * T + 1 + k)
                        nc.gpsimd.tensor_tensor(rstd[:], var[:], half_neg[:], ALU.pow).then_inc(S["rstd_ready"], 1)

        @block.tensor
        def _(pe):
            mm = nc.tensor.matmul
            pe.wait_ge(S["dve_prep"], 1)
            M = ps[:, 7, :]
            for s, h in halves():
                mm(ps[h, 0, 0:64], gain_w[h, 0:64], centre[h, 64 * s:64 * s + 64], start=True, stop=True)
                mm(ps[h, 0, 64:128], gain_w[h, 64:128], centre[h, 64 * s:64 * s + 64], start=True, stop=True)
                mm(ps[h, 0, 128:192], centre[h, 64 * s:64 * s + 64], gain_w[h, 128:192], start=True, stop=True)
                mm(ps[h, 1, 0:HID], centre[h, 64 * s:64 * s + 64], gain_1[h, :], start=True, stop=True)
                for k in range(3):
                    mm(ps[h, 2, k:k + 1], raw_w[h, 64 * k:64 * k + 64], cols[h, B1N:B1N + 1], start=True, stop=True)
            for k in range(HC):
                mm(ps[:, 3, k:k + 1], raw_1[0:64, 128 * k:128 * k + 128], cols[0:64, B2N:B2N + 1],
                   start=True, stop=True)
            for hp in range(2):
                last = nc.tensor.transpose(ps[:, 4, 64 * hp:64 * hp + 64],
                                           bias_t[0:64, 2 * hp:2 * hp + 2, :].rearrange("p h n -> p (h n)"),
                                           ident[0:64, 0:64])
            last.then_inc(S["prep_mm"], 1)
            pe.wait_ge(S["prep_ev"], 1)
            for s, h in halves():
                for hh in range(NH):
                    mm(ps[h, 0, 64 * hh:64 * hh + 64], q_masked[h, hh, :], qk_t[h, 64:128], start=True, stop=True)
                    mm(ps[h, 1, hh:hh + 1], qk_t[h, 64:128], vecs[h, 4 + hh:5 + hh], start=True, stop=True)
                last = mm(ps[h, 2, 0:1], raw_p[h, :], vecs[h, 2:3], start=True, stop=True)
            last.then_inc(S["prep_mm"], 1)
            pe.wait_ge(S["ready"], 1)

            def layer_norm(T, n, src):
                for k in range(NCH):
                    last = mm(ps[:, k, :], centre[:], src(k), start=True, stop=True)
                last.then_inc(S["centred"], 1)
                pe.wait_ge(S["squared"], 2 * T + n + 1)
                for k in range(16):
                    last = mm(ps[:, m_bank, 2 * k:2 * k + 2], sq[:, 128 * k:128 * k + 128], mean_of[:],
                              start=True, stop=True)
                last.then_inc(S["stats"], 1)
                pe.wait_ge(S["rstd_ready"], 2 * T + n + 1)
                nc.tensor.transpose(ps[0:32, m_bank, 128:256], rstd[:], ident[:]).then_inc(S["rstd_tp"], 1)
                pe.wait_ge(S["rstd_copied"], 2 * T + n + 1)
                for k in range(16):
                    last = mm(ps[:, k // 4, 128 * (k % 4):128 * (k % 4) + 128], pick_row[:, k, :], rstd_t[:],
                              start=True, stop=True)
                last.then_inc(S["spread"], 1)
                pe.wait_ge(S["z_ready"], 2 * T + n + 1)

            def hi(ap):
                return ap.bitcast(BF16)[:, 1::2]

            def attention(T):
                gj = 0
                for k in range(NCH):
                    for hh in range(NH):
                        if k:
                            pe.wait_ge(S["u_ready"], 16 * T + 4 * k - 4 + hh + 1)
                        if k and hh == NH - 1:
                            pe.wait_ge(S["v_ready"], 4 * T + k)
                        mm(ps[:, hh, :], w_u[:, hh, :], z1[:, 8 * k:8 * k + 8, :].rearrange("p w t -> p (w t)"),
                           start=True, stop=True).then_inc(S["u_mm"], 1)
                    for w8 in range(8):
                        for s, h in halves():
                            last = mm(ps[h, m_bank, 64 * w8:64 * w8 + 64], z1[h, 8 * k + w8, :], w_v[h, :],
                                      start=True, stop=True)
                    last.then_inc(S["v_mm"], 1)
                    pe.wait_ge(S["u_ready"], 16 * T + 4 * k + 4)
                    if k == 0:
                        pe.wait_ge(S["f_ready"], 4 * T + 1)
                    for hp in range(2):
                        for s, h in halves():
                            if gj >= 2:
                                pe.wait_ge(S["guard_max"], 16 * T + gj - 1)
                            bank = s_bank + gj % 2
                            mm(ps[:, bank, :], ident_bf[:], bias_g[:, hp:hp + 1, :].broadcast_to([128, 8, 64]),
                               start=True, stop=False, skip_group_check=True)
                            for w8 in range(8):
                                last = mm(ps[:, bank, 64 * w8:64 * w8 + 64],
                                          hi(u[h, 8 * k + w8, 2 * hp:2 * hp + 2, :].rearrange("p a n -> p (a n)")),
                                          hi(z1[h, 8 * k + w8, :]), start=False, stop=(w8 == 7),
                                          skip_group_check=True)
                            last.then_inc(S["guard_mm"], 1)
                            gj += 1
                pe.wait_ge(S["v_ready"], 4 * T + 4)
                pe.wait_ge(S["guard_max"], 16 * T + 16)
                nc.tensor.transpose(ps[:, m_bank, 0:64].bitcast(BF16), mx[:], ident_bf[:]).then_inc(S["max_tp"], 1)
                pe.wait_ge(S["max_copied"], T + 1)

                T_BANK = turned_bank

                def scores(r):
                    bank = s_bank + r % 2
                    if r >= 2:
                        pe.wait_ge(S["exp_done"], 16 * T + r - 1)
                    for j in range(3):
                        mm(ps[:, bank, :], ident_bf[:],
                           bias_part[j][:, :, :].rearrange("p h n -> p (h n)").unsqueeze(1).broadcast_to(
                               [128, 2, 256]), start=(j == 0), stop=False, skip_group_check=True)
                    for w2 in range(2):
                        w = 2 * r + w2
                        for hp in range(2):
                            mm(ps[:, bank, 256 * w2 + 128 * hp:256 * w2 + 128 * hp + 128],
                               pick_max[:, w // 8, hp, w % 8, :], mx_t[:], start=False, stop=False,
                               skip_group_check=True)
                        for s, h in halves():
                            last = mm(ps[h, bank, 256 * w2:256 * w2 + 256], z1[h, w, :],
                                      u[h, w, :, :].rearrange("p h n -> p (h n)"), start=False,
                                      stop=True, skip_group_check=True)
                    last.then_inc(S["score_mm"], 1)

                def values(r):
                    pe.wait_ge(S["exp_done"], 16 * T + r + 1)
                    if r:
                        pe.wait_ge(S["o_ready"], 32 * T + 2 * r)
                    for s, h in halves():
                        for w2 in range(2):
                            for hp in range(2):
                                c = 33 * (2 * w2 + hp)
                                last = mm(ps[:, o_bank + s, c:c + 33],
                                          prob[h, r % 4, 256 * w2 + 128 * hp:256 * w2 + 128 * hp + 128],
                                          v[h, 2 * r + w2, hp, :], start=True, stop=True)
                    last.then_inc(S["pv_mm"], 1)

                def turn(r):
                    pe.wait_ge(S["o_ready"], 32 * T + 2 * r + 2)
                    if r % 4 == 0 and 0 < r < 12:
                        pe.wait_ge(S["o_copied"], 4 * T + r // 4)
                    if r == 12:
                        pe.wait_ge(S["x1_ready"], 4 * T + 2)
                    nc.tensor.transpose(ps[:, T_BANK[r // 4], 128 * (r % 4):128 * (r % 4) + 128], o_n[:, r % 2, :],
                                        ident[:]).then_inc(S["o_tp"], 1)

                def project(q):
                    pe.wait_ge(S["o_copied"], 4 * T + q + 1)
                    for w2 in range(2):
                        for h2 in range(2):
                            last = mm(ps[:, q, 256 * w2:256 * w2 + 256], w_p[:, w2, h2, :],
                                      o_t[:, :, 64 * h2:64 * h2 + 64], start=(h2 == 0), stop=(h2 == 1))
                    last.then_inc(S["proj_mm"], 1)

                for r in range(ROUNDS + 3):
                    if r < ROUNDS:
                        scores(r)
                    if 1 <= r <= ROUNDS:
                        values(r - 1)
                    if 2 <= r <= ROUNDS + 1:
                        turn(r - 2)
                    if r >= 6 and (r - 6) % 4 == 0:
                        project((r - 6) // 4)

            def ffn(T):
                def up(k):
                    for s, h in halves():
                        for hc in range(HC):
                            j = 2 * s + hc
                            if k:
                                pe.wait_ge(S["gelu_done"], 16 * T + 4 * (k - 1) + j + 1)
                            mm(ps[:, j, :], w_1[h, 128 * hc:128 * hc + 128], z2[h, BANK * k:BANK * k + BANK],
                               start=True, stop=True).then_inc(S["f1_mm"], 1)

                def down(k):
                    if k >= 2:
                        pe.wait_ge(S["f_ready"], 4 * T + k)
                    for s, h in halves():
                        for hc in range(HC):
                            j = 2 * s + hc
                            pe.wait_ge(S["gelu_done"], 16 * T + 4 * k + j + 1)
                            last = mm(ps[h, s_bank + k % 2, :], w_2[:, hc, :], hid[:, k % 2, j, :],
                                      start=(hc == 0), stop=(hc == HC - 1))
                    last.then_inc(S["f2_mm"], 1)

                for k in range(NCH + 1):
                    if k < NCH:
                        up(k)
                    if k:
                        down(k - 1)

            with pe.Fori(0, PAIRS) as p:
                with pe.Fori(0, TILES) as i:
                    T = p * TILES + i
                    pe.wait_ge(S["x_loaded"], 32 * T + 32)
                    layer_norm(T, 0, lambda k: x_in[:, BANK * k:BANK * k + BANK])
                    attention(T)
                    pe.wait_ge(S["x1_ready"], 4 * T + 5)
                    layer_norm(T, 1, lambda k: x1[:, 2 + 2 * k:4 + 2 * k, 1:257])
                    ffn(T)
                pe.wait_ge(S["flush_done"], p + 1)
                mm(ps[0:G * K2, m_bank, 0:2], conv_w_t[:], mean2[:], start=True, stop=True).then_inc(S["lf_mm"], 1)
                pe.wait_ge(S["lf_dve"], 2 * p + 2)
                for s, h in halves():
                    last = mm(ps[h, m_bank, 64:64 + K2], gsel[:], lf_k[:, s, :], start=True, stop=True)
                last.then_inc(S["lf_mm"], 1)
                pe.wait_ge(S["phase2_ready"], p + 1)

        @block.scalar
        def _(act):
            actf = nc.scalar.activation

            def store_y(p, i, rows):
                for s, h in halves():
                    act.dma_start(y_dram[p + PAIRS * s, :, bass.ds(i * WS, rows), :],
                                  y[h, 0:rows, :]).then_inc(S["y_stored"], 16)

            act.wait_ge(S["ready"], 1)

            def norm_steps(T, n):
                act.wait_ge(S["centred"], 2 * T + n + 1)
                actf(sq[:], wide.rearrange("p a b -> p (a b)"), ACT.Square).then_inc(S["squared"], 1)
                act.wait_ge(S["rstd_tp"], 2 * T + n + 1)
                actf(rstd_t[:], ps[0:32, m_bank, 128:256], ACT.Copy).then_inc(S["rstd_copied"], 1)

            with act.Fori(0, PAIRS) as p:
                with act.Fori(0, TILES) as i:
                    T = p * TILES + i
                    norm_steps(T, 0)
                    for k in range(NCH):
                        for hh in range(NH):
                            act.wait_ge(S["u_mm"], 16 * T + 4 * k + hh + 1)
                            actf(u[:, 8 * k:8 * k + 8, hh, :], ps[:, hh, :].rearrange("p (w n) -> p w n", w=8),
                                 ACT.Identity, bias=b_u[:, hh:hh + 1]).then_inc(S["u_ready"], 1)
                        act.wait_ge(S["v_mm"], 4 * T + k + 1)
                        actf(v[:, 8 * k:8 * k + 8, :, 0:32],
                             ps[:, m_bank, :].rearrange("p (w a d) -> p w a d", w=8, a=2),
                             ACT.Copy).then_inc(S["v_ready"], 1)
                    act.wait_ge(S["max_tp"], T + 1)
                    actf(mx_t[:], ps[:, m_bank, 0:64].bitcast(BF16), ACT.Copy).then_inc(S["max_copied"], 1)

                    def copy_o(q):
                        act.wait_ge(S["o_tp"], 16 * T + 4 * q + 4)
                        if q:
                            act.wait_ge(S["proj_mm"], 4 * T + q)
                        actf(o_t[:, :, :].rearrange("p a b -> p (a b)"), ps[:, turned_bank[q], :],
                             ACT.Copy).then_inc(S["o_copied"], 1)

                    for r in range(ROUNDS):
                        act.wait_ge(S["score_mm"], 16 * T + r + 1)
                        if r >= 4:
                            act.wait_ge(S["pv_mm"], 16 * T + r - 3)
                        actf(prob[:, r % 4, :], ps[:, s_bank + r % 2, :], ACT.Exp).then_inc(S["exp_done"], 1)
                        if r >= 6 and (r - 6) % 4 == 0:
                            copy_o((r - 6) // 4)
                    copy_o(3)
                    act.wait_ge(S["conv_done"], T + 1)
                    actf(y[:, 0, :], f[:, 0, :], ACT.Identity, bias=b_y[:, 0:1],
                         accum_out=acc[:, 0:1])
                    actf(y[:, 1:WS, :], f[:, 1:WS, :], ACT.Identity, bias=b_y[:, 0:1],
                         accum_out=acc[:, 1:2]).then_inc(S["y_done"], 1)
                    act.wait_ge(S["y_done"], T + 1)
                    store_y(p, i, WS)
                    norm_steps(T, 1)
                    for k in range(NCH):
                        if k >= 2:
                            act.wait_ge(S["f2_mm"], 4 * T + k - 1)
                        for j in range(4):
                            act.wait_ge(S["f1_mm"], 16 * T + 4 * k + j + 1)
                            actf(hid[:, k % 2, j, :], ps[:, j, :], ACT.Gelu,
                                 bias=b_1[:, j % HC:j % HC + 1]).then_inc(S["gelu_done"], 1)
                    act.wait_ge(S["y_stored"], 32 * (T + p * 2 + 1))
                act.wait_ge(S["flush_step"], 2 * p + 1)
                actf(y[:, 0, :], f[:, 0, :], ACT.Identity, bias=b_y[:, 0:1], accum_out=acc[:, 0:1])
                actf(y[:, 1:WS, :], f[:, 1:WS, :], ACT.Identity, bias=b_y[:, 0:1],
                     accum_out=acc[:, 1:2]).then_inc(S["lf_act"], 1)
                act.wait_ge(S["lf_act"], 3 * p + 1)
                store_y(p, TILES, WS)
                act.wait_ge(S["y_stored"], 32 * ((p + 1) * (TILES + 2) - 1))
                act.wait_ge(S["flush_step"], 2 * p + 2)
                actf(y[:, 0, :], f[:, WS, :], ACT.Identity, bias=b_y[:, 0:1],
                     accum_out=acc[:, 0:1]).then_inc(S["lf_act"], 1)
                act.wait_ge(S["lf_act"], 3 * p + 2)
                store_y(p, TILES + 1, 1)
                act.wait_ge(S["y_stored"], 32 * (p + 1) * (TILES + 2))
                act.wait_ge(S["lf_dve"], 2 * p + 1)
                actf(lf[:], lf[:], ACT.Tanh).then_inc(S["lf_act"], 1)

                def second(n, N, i):
                    act.wait_ge(S[f"y_loaded{n}"], 32 * N + 32)
                    actf(res[:, n, :, :], y_in[:, n, 1:9, 1:257], ACT.Identity, bias=const1[:, 0:1],
                         scale=taps1[:, 4:5]).then_inc(S[f"tap_first{n}"], 1)

                def store(n, N, i):
                    act.wait_ge(S[f"res_done{n}"], N + 1)
                    for s, h in halves():
                        act.dma_start(out[p + PAIRS * s, :, bass.ds(i * WS, WS), :],
                                      res[h, n, :, :]).then_inc(S[f"out_stored{n}"], 16)

                act.wait_ge(S["phase2_ready"], p + 1)
                with act.Fori(0, TILES // 2) as j:
                    N = p * (TILES // 2) + j
                    second(0, N, 2 * j)
                    second(1, N, 2 * j + 1)
                    store(0, N, 2 * j)
                    store(1, N, 2 * j + 1)
                    act.wait_ge(S["out_stored0"], 32 * N + 32)
                    act.wait_ge(S["out_stored1"], 32 * N + 32)
                act.wait_ge(S["out_stored1"], 32 * (TILES // 2) * (p + 1))

        @block.vector
        def _(dve):
            V = nc.vector
            step = [0]

            def chain(ins):
                step[0] += 1
                ins.then_inc(S["dve_chain"], 1)
                dve.wait_ge(S["dve_chain"], step[0])

            chain(V.memset(w_p[:].rearrange("p a b c -> p (a b c)"), 0.0))
            V.memset(w_u[:].rearrange("p a b -> p (a b)"), 0.0).then_inc(S["z_init"], 1)
            chain(V.memset(x1[:].rearrange("p a b -> p (a b)"), 0.0))
            chain(V.memset(v[:, :, :, 32:33], 1.0))
            chain(V.memset(f[:].rearrange("p a b -> p (a b)"), 0.0))
            dve.wait_ge(S["const_loaded"], n_const[0])
            chain(V.tensor_copy(ident_bf[:], ident[:]))
            chain(V.tensor_copy(pick_row[:].rearrange("r k (s c) -> r (k s) c", s=2),
                                ident[0:32, 0:32].unsqueeze(2).broadcast_to([32, 32, 64])))
            for k in range(NCH):
                for hp in range(2):
                    for s in range(2):
                        i0 = 32 * k + 16 * hp + 8 * s
                        V.tensor_scalar(pick_max[:, k, hp, :, 64 * s:64 * s + 64],
                                        ident[:, i0:i0 + 8].unsqueeze(2).broadcast_to([128, 8, 64]),
                                        -1.0, None, ALU.mult)
            chain(V.tensor_copy(bias_part[0][:], bias_t[:]))
            rest = sq[:, 0:256].rearrange("p (h n) -> p h n", h=NH)
            chain(V.tensor_tensor(rest, bias_t[:], bias_part[0][:], ALU.subtract))
            chain(V.tensor_copy(bias_part[1][:], rest))
            chain(V.tensor_tensor(rest, rest, bias_part[1][:], ALU.subtract))
            chain(V.tensor_copy(bias_part[2][:], rest))
            chain(V.tensor_scalar(gain_w[:], raw_w[:], cols[:, G1:G1 + 1], None, ALU.mult))
            V.tensor_scalar(gain_1[:], raw_1[:], cols[:, G2:G2 + 1], None, ALU.mult).then_inc(S["dve_prep"], 1)
            dve.wait_ge(S["prep_mm"], 1)
            chain(V.tensor_copy(qk_t[:], ps[:, 0, 0:128]))
            chain(V.tensor_copy(w_v[:], ps[:, 0, 128:192]))
            chain(V.tensor_copy(w_1[:], ps[:, 1, 0:HID]))
            chain(V.tensor_tensor(vecs[:, 0:1], ps[:, 2, 0:1], cols[:, QB:QB + 1], ALU.add))
            chain(V.tensor_tensor(vecs[:, 2:3], ps[:, 2, 2:3], cols[:, VB:VB + 1], ALU.add))
            chain(V.tensor_tensor(b_1[:], b_1[:], ps[:, 3, 0:HC], ALU.add))
            chain(V.tensor_copy(bias_g[:], ps[:, 4, 0:128].rearrange("p (a m) -> p a m", a=2)))
            for hh in range(NH):
                chain(V.tensor_scalar(q_masked[:, hh, :], qk_t[:, 0:64], headmask[:, hh:hh + 1], None, ALU.mult))
            chain(V.tensor_scalar(vecs[:, 4:8], headmask[:], vecs[:, 0:1], None, ALU.mult))
            V.memset(vecs[:, 8:9], 0.0).then_inc(S["prep_ev"], 1)
            dve.wait_ge(S["prep_mm"], 2)
            for s, h in halves():
                chain(V.tensor_copy(w_u[h, :, 64 * s:64 * s + 64],
                                    ps[h, 0, 0:256].rearrange("p (h c) -> p h c", h=NH)))
            chain(V.tensor_copy(b_u[:], ps[:, 1, 0:NH]))
            chain(V.tensor_tensor(b_p[:], ps[:, 2, 0:1], cols[:, PB:PB + 1], ALU.add))
            chain(V.tensor_tensor(b_y[:], cols[:, FB:FB + 1], cols[:, DB:DB + 1], ALU.add))
            chain(V.tensor_scalar(taps0[:, 4:5], taps0[:, 4:5], 1.0, None, ALU.add))
            chain(V.scalar_tensor_tensor(l1c[:, 3:4], l1c[:, 2:3], 1.0, l1c[:, 0:1], ALU.add, ALU.mult))
            chain(V.tensor_scalar(l1c[:, 4:5], l1c[:, 1:2], 1.0, None, ALU.add))
            chain(V.scalar_tensor_tensor(l1c[:, 5:6], l1c[:, 2:3], -1.0, l1c[:, 0:1], ALU.mult, ALU.mult))
            V.tensor_scalar(bn[:, 6:7], bn[:, 3:4], BN_EPS, None, ALU.add).then_inc(S["bn_var"], 1)
            V.memset(tot[:], 0.0).then_inc(S["f_ready"], 1)
            V.memset(flags[:], 0.0).then_inc(S["x1_ready"], 1)
            dve.wait_ge(S["bn_root"], 1)
            chain(V.tensor_tensor(bn[:, 4:5], bn[:, 0:1], bn[:, 7:8], ALU.mult))
            chain(V.tensor_tensor(bn[:, 6:7], bn[:, 2:3], bn[:, 4:5], ALU.mult))
            chain(V.tensor_tensor(bn[:, 5:6], bn[:, 1:2], bn[:, 6:7], ALU.subtract))
            V.memset(acc[:], 0.0).then_inc(S["ready"], 1)

            def norm_apply(T, n):
                dve.wait_ge(S["stats"], 2 * T + n + 1)
                V.tensor_scalar(var[:], ps[:, m_bank, 0:32], LN_EPS, None, ALU.add).then_inc(S["var_ready"], 1)
                dve.wait_ge(S["spread"], 2 * T + n + 1)
                if n == 0:
                    V.tensor_tensor(z1[:].rearrange("p w (r c) -> p r w c", r=WS),
                                    x_in[:].rearrange("p (r w c) -> p r w c", r=WS, c=WS),
                                    wide.rearrange("p a b -> p (a b)").rearrange("p (r w c) -> p r w c", r=WS, c=WS),
                                    ALU.mult).then_inc(S["z_ready"], 1)
                else:
                    V.tensor_tensor(z2[:].rearrange("p (r w) -> p r w", r=WS), x1[:, 2:10, 1:257],
                                    wide.rearrange("p a b -> p (a b)").rearrange("p (r w) -> p r w", r=WS),
                                    ALU.mult).then_inc(S["z_ready"], 1)

            def residual(T, q):
                dve.wait_ge(S["proj_mm"], 4 * T + q + 1)
                dve.wait_ge(S["xb_ready"], T + 1)
                for w2 in range(2):
                    w0 = 8 * q + w2
                    last = V.tensor_tensor(
                        x1[:, 2:10, 1:257].rearrange("p r (w c) -> p w r c", c=WS)[:, w0:w0 + 7:2, :, :],
                        ps[:, q, 256 * w2:256 * w2 + 256].rearrange("p (w r c) -> p w r c", w=4, r=WS),
                        xb[:].rearrange("p (r w c) -> p w r c", r=WS, c=WS)[:, w0:w0 + 7:2, :, :],
                        ALU.add)
                last.then_inc(S["x1_ready"], 1)

            TAPS = [t for t in range(K2) if t != 4]

            def conv_tap(n, rows, src, dst, wait):
                t = TAPS[n]
                return V.scalar_tensor_tensor(dst, src[:, t // 3:t // 3 + rows, t % 3:t % 3 + IMG],
                                              wait[:, t:t + 1], dst, ALU.mult, ALU.add)

            with dve.Fori(0, PAIRS) as p:
                with dve.Fori(0, TILES) as i:
                    T = p * TILES + i
                    norm_apply(T, 0)
                    for k in range(NCH):
                        for gj in range(4):
                            n = 4 * k + gj
                            dve.wait_ge(S["guard_mm"], 16 * T + n + 1)
                            V.tensor_reduce(mx[:, 8 * n:8 * n + 8],
                                            ps[:, s_bank + n % 2, :].rearrange("p (w m) -> p w m", w=8),
                                            AX.X, ALU.max).then_inc(S["guard_max"], 1)
                    for r in range(ROUNDS):
                        dve.wait_ge(S["pv_mm"], 16 * T + r + 1)
                        O = ps[:, o_bank:o_bank + 2, 0:132].rearrange("p s (g d) -> p s g d", d=33)
                        V.reciprocal(rsum[:, r % 2, :].rearrange("p (s g) -> p s g", s=2), O[:, :, :, 32]).then_inc(
                            S["o_recip"], 1)
                        dve.wait_ge(S["o_recip"], 16 * T + r + 1)
                        if r >= 2:
                            dve.wait_ge(S["o_tp"], 16 * T + r - 1)
                        for h2, h in halves():
                            V.tensor_tensor(o_n[h, r % 2, :].rearrange("p (s g d) -> p s g d", s=2, d=HD),
                                            O[h, :, :, 16 * h2:16 * h2 + 16],
                                            rsum[h, r % 2, :].rearrange("p (s g) -> p s g", s=2).unsqueeze(3)
                                            .broadcast_to([64, 2, 4, HD]),
                                            ALU.mult).then_inc(S["o_ready"], 1)
                        if r < 8:
                            ins = conv_tap(r, WS, x1, f[:, 0:WS, :], taps0)
                            if r < 7:
                                ins.then_inc(S["conv_step"], 1)
                                dve.wait_ge(S["conv_step"], 9 * T + r + 1)
                            else:
                                ins.then_inc(S["conv_done"], 1)
                                dve.wait_ge(S["conv_done"], T + 1)
                        if r == 9:
                            V.tensor_copy(x1[:, 0:2, :], x1[:, 8:10, :]).then_inc(S["conv_step"], 1)
                            dve.wait_ge(S["conv_step"], 9 * T + 8)
                        if r in (11, 13, 15):
                            residual(T, (r - 11) // 2)
                    residual(T, 3)
                    dve.wait_ge(S["y_done"], T + 1)
                    V.scalar_tensor_tensor(tot[:], acc[:, 0:1], flags[:, 0:1], tot[:], ALU.mult, ALU.add).then_inc(
                        S["tot_step"], 1)
                    dve.wait_ge(S["tot_step"], 4 * T + 1)
                    V.scalar_tensor_tensor(tot[:], acc[:, 1:2], flags[:, 1:2], tot[:], ALU.mult, ALU.add).then_inc(
                        S["tot_step"], 1)
                    V.tensor_copy(flags[:, 0:1], flags[:, 1:2]).then_inc(S["tot_step"], 1)
                    V.tensor_copy(f[:, 0, :], f[:, WS, :]).then_inc(S["conv_step"], 1)
                    dve.wait_ge(S["conv_step"], 9 * T + 9)
                    dve.wait_ge(S["tot_step"], 4 * T + 3)
                    V.memset(flags[:, 1:2], 1.0).then_inc(S["tot_step"], 1)
                    dve.wait_ge(S["tot_step"], 4 * T + 4)
                    norm_apply(T, 1)
                    for k in range(NCH):
                        dve.wait_ge(S["f2_mm"], 4 * T + k + 1)
                        V.scalar_tensor_tensor(f[:, 1 + 2 * k:3 + 2 * k, :], x1[:, 2 + 2 * k:4 + 2 * k, 1:257],
                                               taps0[:, 4:5],
                                               ps[:, s_bank + k % 2, :].rearrange("p (r w) -> p r w", r=2),
                                               ALU.mult, ALU.add).then_inc(S["f_ready"], 1)
                n_fl = [0]

                def flush(ins):
                    n_fl[0] += 1
                    ins.then_inc(S["flush_chain"], 1)
                    dve.wait_ge(S["flush_chain"], FLUSH_STEPS * p + n_fl[0])

                dve.wait_ge(S["f_ready"], 4 * TILES * (p + 1) + 1)
                for n in range(7):
                    flush(conv_tap(n, WS, x1, f[:, 0:WS, :], taps0))
                conv_tap(7, WS, x1, f[:, 0:WS, :], taps0).then_inc(S["flush_step"], 1)
                flush(V.tensor_copy(x1[:, 0:2, :], x1[:, 8:10, :]))
                flush(V.memset(x1[:, 2, :], 0.0))
                for n in range(7):
                    flush(conv_tap(n, 1, x1, f[:, WS:WS + 1, :], taps0))
                dve.wait_ge(S["lf_act"], 3 * p + 1)
                flush(V.tensor_tensor(tot[:], tot[:], acc[:, 0:1], ALU.add))
                flush(V.tensor_tensor(tot[:], tot[:], acc[:, 1:2], ALU.add))
                conv_tap(7, 1, x1, f[:, WS:WS + 1, :], taps0).then_inc(S["flush_step"], 1)
                dve.wait_ge(S["lf_act"], 3 * p + 2)
                flush(V.tensor_tensor(tot[:], tot[:], acc[:, 0:1], ALU.add))
                flush(V.tensor_scalar(tot[:], tot[:], 1.0 / (IMG * IMG), None, ALU.mult))
                V.tensor_scalar(mean2[:], mean_of[:], tot[:, 0:1], float(C), ALU.mult, ALU.mult).then_inc(
                    S["flush_done"], 1)
                dve.wait_ge(S["lf_mm"], 2 * p + 1)
                V.tensor_scalar(lf[:], ps[0:G * K2, m_bank, 0:2], bn[:, 4:5], bn[:, 5:6], ALU.mult,
                                ALU.add).then_inc(S["lf_dve"], 1)
                dve.wait_ge(S["lf_act"], 3 * p + 3)
                V.tensor_scalar(lf_k[:, 0, :], kmask[:], lf[:, 0:1], None, ALU.mult)
                V.tensor_scalar(lf_k[:, 1, :], kmask[:], lf[:, 1:2], None, ALU.mult).then_inc(S["lf_dve"], 1)
                dve.wait_ge(S["lf_mm"], 2 * p + 2)
                flush(V.tensor_scalar(taps1[:], ps[:, m_bank, 64:64 + K2], l1c[:, 3:4], None, ALU.mult))
                flush(V.tensor_tensor(taps1[:, 4:5], taps1[:, 4:5], l1c[:, 4:5], ALU.add))
                flush(V.tensor_tensor(const1[:], tot[:], l1c[:, 5:6], ALU.mult))
                flush(V.memset(tot[:], 0.0))
                flush(V.memset(flags[:], 0.0))
                flush(V.memset(f[:].rearrange("p a b -> p (a b)"), 0.0))
                V.memset(x1[:].rearrange("p a b -> p (a b)"), 0.0).then_inc(S["phase2_ready"], 1)
                assert n_fl[0] == FLUSH_STEPS
                with dve.Fori(0, TILES // 2) as j:
                    N = p * (TILES // 2) + j
                    for n in range(2):
                        dve.wait_ge(S[f"y_loaded{n}"], 32 * N + 32)
                        V.tensor_copy(y_in[:, n, :, 0:1], y_in[:, n, :, 2:3]).then_inc(S["edge_done"], 1)
                        V.tensor_copy(y_in[:, n, :, 257:258], y_in[:, n, :, 255:256]).then_inc(S["edge_done"], 1)
                        dve.wait_ge(S["edge_done"], 4 * N + 2 * n + 2)
                        dve.wait_ge(S[f"tap_first{n}"], N + 1)
                        for k in range(8):
                            ins = conv_tap(k, WS, y_in[:, n, :, :], res[:, n, :, :], taps1)
                            if k < 7:
                                ins.then_inc(S[f"tap_step{n}"], 1)
                                dve.wait_ge(S[f"tap_step{n}"], 7 * N + k + 1)
                            else:
                                ins.then_inc(S[f"res_done{n}"], 1)


_INS = ["qkv_w", "proj_w", "ffn_w1", "ffn_w2", "qkv_b", "proj_b", "norm1_g", "norm1_b", "norm2_g", "norm2_b",
        "ffn_b1", "ffn_w2_b", "dw_w", "dw_b"]
_INS1 = ["conv_w", "bn_gamma", "bn_beta", "bn_mean", "bn_var", "lamb_l", "lamb_h", "inside_all"]


def constants():
    import numpy as np
    f = np.float32
    two = np.kron(np.eye(2, dtype=f), np.ones((C, 1), f))
    c = np.eye(C, dtype=f) - f(1.0 / C)
    g = np.arange(G * K2) // K2
    return {
        "c_ident": np.eye(128, dtype=f),
        "c_centre": np.kron(np.eye(2, dtype=f), c),
        "c_mean": two / f(C),
        "c_head": np.kron(np.ones((2, 1), f), np.kron(np.eye(NH, dtype=f), np.ones((HD, 1), f))) * f(HD ** -0.5),
        "c_gsel": (g[:, None] == (np.arange(C) // (C // G))[None, :]).astype(f),
        "c_kmask": (np.arange(G * K2)[:, None] % K2 == np.arange(K2)[None, :]).astype(f),
    }


def kernel(**inputs):
    import numpy as _np
    import concourse.bacc as _bacc
    from concourse import mybir as _mybir
    from concourse.bass_utils import run_bass_kernel_spmd as _run

    nc = _bacc.Bacc("TRN2", target_bir_lowering=False, num_devices=1)
    arrays = {"x": _np.ascontiguousarray(inputs["x"])}
    for name in _INS:
        arrays[name] = _np.ascontiguousarray(inputs["L0_conv_" + name])
    for name in _INS1:
        arrays[name] = _np.ascontiguousarray(inputs["L1_conv_" + name])
    arrays["rpb_t"] = _np.ascontiguousarray(_np.asarray(inputs["L0_conv_rpb_table"]).T)
    arrays.update(constants())
    arrays = {"in_" + n: v for n, v in arrays.items()}
    aps = {n[3:]: nc.dram_tensor(n, v.shape, _mybir.dt.from_np(v.dtype), kind="ExternalInput").ap()
           for n, v in arrays.items()}
    out = nc.dram_tensor("out_0", arrays["in_x"].shape, _mybir.dt.float32, kind="ExternalOutput").ap()
    bass_window_block(nc, aps, out)
    r = _run(nc, [arrays], core_ids=[0])
    return r.results[0]["out_0"]
```

```python
from contextlib import ExitStack

import concourse.bass as bass
from concourse import mybir

F32 = mybir.dt.float32
BF16 = mybir.dt.bfloat16
F16 = mybir.dt.float16
ALU = mybir.AluOpType
ACT = mybir.ActivationFunctionType
AX = mybir.AxisListType

C = 64
WS = 8
NH = 4
HD = C // NH
HID = 256
IMG = 256
B = 8
PAIRS = B // 2
TILES = IMG // WS
TOK = WS * IMG
NW = IMG // WS
BANK = 512
NCH = TOK // BANK
ROUNDS = NW // 2
LN_EPS = 1e-5
BN_EPS = 1e-5
G = 8
K2 = 9
YROWS = 10 + IMG
Y0 = 9
HC = HID // 128
FLUSH_STEPS = 3 + 2 + 7 + 2 + 2 + 3 + 3
HALF = WS // 2
CONV_STEPS = 8 + 1 + 8


def halves():
    return ((0, slice(0, 64)), (1, slice(64, 128)))


def bass_window_block(nc, a, out):
    with ExitStack() as ctx:
        def sb(name, shape, dt=F32):
            return ctx.enter_context(nc.sbuf_tensor(name, shape, dt))

        def sem(name):
            return ctx.enter_context(nc.semaphore(name))

        ident = sb("ident", [128, 128])
        ident_bf = sb("ident_bf", [128, 128], BF16)
        centre = sb("centre", [128, 128])
        mean_of = sb("mean_of", [128, 2])
        headmask = sb("headmask", [128, NH])
        gsel = sb("gsel", [G * K2, C])
        kmask = sb("kmask", [G * K2, K2])
        mean_all = sb("mean_all", [128, 128])
        pick_row = sb("pick_row", [96, 16, 128], BF16)
        pick_max = sb("pick_max", [128, NCH, 2, 8, 128], BF16)
        w_u = sb("w_u", [128, NH, 128])
        b_u = sb("b_u", [128, NH])
        w_v = sb("w_v", [128, C])
        w_p = sb("w_p", [128, 2, 2, 128])
        b_p = sb("b_p", [128, 1])
        w_1 = sb("w_1", [128, HID])
        b_1 = sb("b_1", [128, HC])
        w_2 = sb("w_2", [128, HC, C])
        b_y = sb("b_y", [128, 1])
        taps0 = sb("taps0", [128, K2])
        bias_t = sb("bias_t", [128, NH, 64])
        bias_s = sb("bias_s", [128, NH, 64], F16)
        twice = sb("twice", [128, 128], F16)
        bias_g = sb("bias_g", [128, 2, 64], BF16)
        cols = sb("cols", [128, 16])
        raw_w = sb("raw_w", [128, 3 * C])
        raw_p = sb("raw_p", [128, C])
        raw_1 = sb("raw_1", [128, HID])
        gain_w = sb("gain_w", [128, 3 * C])
        gain_1 = sb("gain_1", [128, HID])
        qk_t = sb("qk_t", [128, 2 * C])
        q_masked = sb("q_masked", [128, NH, C])
        vecs = sb("vecs", [128, 12])
        conv_w_t = sb("conv_w_t", [128, G * K2])
        bn = sb("bn", [G * K2, 8])
        lf = sb("lf", [G * K2, 2])
        lf_k = sb("lf_k", [G * K2, 2, K2])
        taps1 = sb("taps1", [128, K2])
        l1c = sb("l1c", [128, 8])
        const1 = sb("const1", [128, 1])
        half_neg = sb("half_neg", [128, 32])

        x_in = sb("x_in", [128, TOK])
        xb = sb("xb", [128, TOK])
        sq = sb("sq", [128, TOK])
        z1 = sb("z1", [128, NW, 64])
        z_bd = sb("z_bd", [128, NW, 128])
        u = sb("u", [128, NW, NH, 64])
        v = sb("v", [128, NW, 2, 2, 33])
        var = sb("var", [128, 32])
        rstd = sb("rstd", [128, 32])
        rstd3 = sb("rstd3", [128, 96], BF16)
        rstd_t = sb("rstd_t", [96, 128], BF16)
        zero32 = sb("zero32", [128, 32])
        mx = sb("mx", [128, 128], BF16)
        mx_t = sb("mx_t", [128, 128], BF16)
        rsum = sb("rsum", [128, 2, 8])
        o_n = sb("o_n", [128, 2, 128])
        o_t = sb("o_t", [128, 4, 128])
        x1 = sb("x1", [128, WS + 2, IMG + 2])
        z2 = sb("z2", [128, TOK])
        hid = sb("hid", [128, 2, 4, BANK])
        prob = hid[:, 0, :, :]
        f = sb("f", [128, WS + 1, IMG])
        acc = sb("acc", [128, 2])
        tot = sb("tot", [128, 1])
        mean2 = sb("mean2", [128, 2])
        flags = sb("flags", [128, 2])
        y_in = sb("y_in", [128, WS + 2, IMG + 2])
        res = sb("res", [128, WS, IMG])
        y_end = u[:, :, :, :].rearrange("p a b c -> p (a b c)")[:, 0:2 * 10 * 258].rearrange(
            "p (n r w) -> p n r w", n=2, r=10)
        res_end = hid[:, :, :, :].rearrange("p n j t -> p n (j t)").rearrange("p n (r w) -> p n r w", w=IMG)

        ps = ctx.enter_context(nc.psum_tensor("ps", [128, 8, BANK], F32))
        stat_bank, proj_bank, s_bank, o_bank, t_bank = 2, 3, 4, 6, 7
        m_bank = stat_bank
        u_banks = (7, 3)
        f_banks = (2, 3, 6, 7)

        y_dram = nc.dram_tensor("y_scratch", [B, C, YROWS, IMG], F32, kind="Internal").ap()

        names = """const_loaded prep_mm prep_ev dve_chain dve_prep bn_root bn_var flush_chain pool_prep ready z_init
            x_loaded ln_mm ln_read squared stats var_ready rstd_ready pool_step rstd_tp rstd_copied
            zbd_ready u_mm u_ready guard_mm guard_max v_mm v_ready max_tp max_copied
            score_mm exp_done pv_mm o_recip o_ready o_tp o_copied proj_mm xb_ready x1_ready f1_mm gelu_done f2_mm
            f_ready conv_step f_shift f_centre y_done y_stored tot_step flush_step flush_done lf_mm lf_act lf_dve
            phase2_ready row_fix y_loaded edge_done tap_first tap_step res_done out_stored
            e_loaded0 e_loaded1 e_edge0 e_edge1 e_first0 e_first1 e_step0 e_step1 e_done0 e_done1
            e_stored0 e_stored1""".split()
        S = {n: sem(n) for n in names}

        xv = a["x"].rearrange("b c (i h) w -> b i c (h w)", h=WS)
        ctx.enter_context(nc.allow_non_contiguous_dma(reason="small weights"))
        block = ctx.enter_context(nc.Block())

        QB, PB, G1, B1N, G2, B2N, FB, DB, VB, KB = range(10)

        n_const = [0]

        @block.sync
        def _(sp):
            def ld(dst, src):
                sp.dma_start(dst, src).then_inc(S["const_loaded"], 16)
                n_const[0] += 16

            ld(ident[:], a["c_ident"])
            ld(centre[:], a["c_centre"])
            ld(mean_of[:], a["c_mean"])
            ld(headmask[:], a["c_head"])
            ld(gsel[:], a["c_gsel"])
            ld(kmask[:], a["c_kmask"])
            qkv_b = a["qkv_b"].rearrange("(k c o) -> k c o", k=3, o=1)

            def column(name):
                return a[name].rearrange("(c o) -> c o", o=1)

            for s, h in halves():
                ld(raw_w[h, :], a["qkv_w"])
                ld(raw_p[h, :], a["proj_w"])
                ld(raw_1[h, :], a["ffn_w1"])
                for k, src in ((QB, qkv_b[0]), (KB, qkv_b[1]), (VB, qkv_b[2]), (PB, column("proj_b")),
                               (G1, column("norm1_g")), (B1N, column("norm1_b")), (G2, column("norm2_g")),
                               (B2N, column("norm2_b")), (FB, column("ffn_w2_b")), (DB, column("dw_b"))):
                    ld(cols[h, k:k + 1], src)
                ld(taps0[h, :], a["dw_w"].rearrange("c o i j -> c (o i j)"))
                ld(l1c[h, 0:1], column("lamb_l"))
                ld(l1c[h, 1:2], column("lamb_h"))
                ld(l1c[h, 2:3], a["inside_all"].rearrange("c a b -> c (a b)"))
                ld(conv_w_t[h, :], a["conv_w"].rearrange("g c -> c g"))
            ld(b_1[:], a["ffn_b1"].rearrange("(k p) -> p k", k=HC))
            ld(w_2[:], a["ffn_w2"].rearrange("(k p) c -> p k c", k=HC))
            for k, name in enumerate(("bn_gamma", "bn_beta", "bn_mean", "bn_var")):
                ld(bn[:, k:k + 1], column(name))
            tab = a["rpb_t"]
            for m in range(64):
                r0, c0 = WS - 1 - m // WS, WS - 1 - m % WS
                for s in range(2):
                    src = tab.rearrange("h (r c) -> h r c", c=2 * WS - 1)[:, r0:r0 + WS, c0:c0 + WS]
                    ld(bias_t[64 * s + m:64 * s + m + 1, :, :].rearrange("p h (r c) -> p h r c", c=WS),
                       src.rearrange("(o h) r c -> o h r c", o=1))
            sp.wait_ge(S["z_init"], 1)
            for w in range(2):
                for h2 in range(2):
                    for s in range(2):
                        for hp in range(2):
                            p0 = 64 * w + 32 * hp + 16 * s
                            ld(w_p[p0:p0 + 16, w, h2, 64 * s:64 * s + 64],
                               a["proj_w"][HD * (2 * hp + h2):HD * (2 * hp + h2 + 1), :])

            def load_x(p, i):
                for s, h in halves():
                    sp.dma_start(x_in[h, :], xv[p + PAIRS * s, i, :, :]).then_inc(S["x_loaded"], 16)

            def fix_rows(p):
                sp.wait_ge(S["y_stored"], (p + 1) * 32 * (TILES + 2))
                for s in range(2):
                    yb = y_dram[p + PAIRS * s, :, :, :]
                    sp.dma_start(yb[:, Y0 - 1, :], yb[:, Y0 + 1, :]).then_inc(S["row_fix"], 16)
                    sp.dma_start(yb[:, Y0 + IMG, :], yb[:, Y0 + IMG - 2, :]).then_inc(S["row_fix"], 16)
                sp.wait_ge(S["row_fix"], (p + 1) * 64)

            def load_y(p, i, dst, signal):
                for s, h in halves():
                    sp.dma_start(dst[h, :, 1:257], y_dram[p + PAIRS * s, :, bass.ds(i * WS + Y0 - 1, WS + 2), :]
                                 ).then_inc(S[signal], 16)

            def store_res(p, i, src, signal):
                for s, h in halves():
                    sp.dma_start(out[p + PAIRS * s, :, bass.ds(i * WS, WS), :], src[h, :, :]).then_inc(S[signal], 16)

            def x_after(T, p, i):
                sp.wait_ge(S["xb_ready"], T + 2)
                sp.wait_ge(S["ln_read"], 16 * T + 12)
                load_x(p, i)

            def out_tile(N, p, i, more):
                sp.wait_ge(S["res_done"], N + 1)
                store_res(p, i, res, "out_stored")
                sp.wait_ge(S["out_stored"], 32 * N + 32)
                if more:
                    load_y(p, i + 1, y_in, "y_loaded")

            load_x(0, 0)
            sp.wait_ge(S["xb_ready"], 1)
            sp.wait_ge(S["ln_read"], 4)
            load_x(0, 1)
            with sp.Fori(0, TILES - 2) as i:
                x_after(i, 0, i + 2)
            x_after(TILES - 2, 1, 0)
            x_after(TILES - 1, 1, 1)
            fix_rows(0)
            load_y(0, 0, y_in, "y_loaded")
            with sp.Fori(1, PAIRS - 1) as p:
                with sp.Fori(0, TILES - 2) as i:
                    x_after(p * TILES + i, p, i + 2)
                    out_tile((p - 1) * TILES + i, p - 1, i, True)
                x_after(p * TILES + TILES - 2, p + 1, 0)
                out_tile((p - 1) * TILES + TILES - 2, p - 1, TILES - 2, True)
                x_after(p * TILES + TILES - 1, p + 1, 1)
                out_tile((p - 1) * TILES + TILES - 1, p - 1, TILES - 1, False)
                fix_rows(p)
                load_y(p, 0, y_in, "y_loaded")
            P3 = PAIRS - 1
            with sp.Fori(0, TILES - 2) as i:
                x_after(P3 * TILES + i, P3, i + 2)
                out_tile((P3 - 1) * TILES + i, P3 - 1, i, True)
            x_after(P3 * TILES + TILES - 2, 0, 0)
            out_tile((P3 - 1) * TILES + TILES - 2, P3 - 1, TILES - 2, True)
            out_tile((P3 - 1) * TILES + TILES - 1, P3 - 1, TILES - 1, False)
            fix_rows(P3)
            sp.wait_ge(S["phase2_ready"], PAIRS)
            for n in range(2):
                load_y(P3, n, y_end[:, n, :, :], f"e_loaded{n}")
            with sp.Fori(0, TILES // 2 - 1) as j:
                for n in range(2):
                    sp.wait_ge(S[f"e_done{n}"], j + 1)
                    load_y(P3, 2 * j + 2 + n, y_end[:, n, :, :], f"e_loaded{n}")
            sp.wait_ge(S["out_stored"], 32 * TILES * P3)

        @block.gpsimd
        def _(pool):
            add, sub = ALU.add, ALU.subtract
            nc.gpsimd.memset(half_neg[:], -0.5).then_inc(S["pool_prep"], 1)
            nc.gpsimd.memset(zero32[:], 0.0).then_inc(S["pool_prep"], 1)
            pool.wait_ge(S["pool_prep"], 2)
            pool.wait_ge(S["bn_var"], 1)
            nc.gpsimd.tensor_tensor(bn[:, 7:8], bn[:, 6:7], half_neg[0:G * K2, 0:1], ALU.pow).then_inc(S["bn_root"], 1)
            pool.wait_ge(S["ready"], 1)

            def root(n):
                tt = nc.gpsimd.tensor_tensor
                pool.wait_ge(S["var_ready"], n)
                tt(rstd[:], var[:], half_neg[:], ALU.pow).then_inc(S["pool_step"], 1)
                pool.wait_ge(S["pool_step"], 5 * n - 4)
                tt(rstd3[:, 0:32], rstd[:], zero32[:], add).then_inc(S["pool_step"], 1)
                pool.wait_ge(S["pool_step"], 5 * n - 3)
                tt(rstd[:], rstd[:], rstd3[:, 0:32], sub).then_inc(S["pool_step"], 1)
                pool.wait_ge(S["pool_step"], 5 * n - 2)
                tt(rstd3[:, 32:64], rstd[:], zero32[:], add).then_inc(S["pool_step"], 1)
                pool.wait_ge(S["pool_step"], 5 * n - 1)
                tt(rstd[:], rstd[:], rstd3[:, 32:64], sub).then_inc(S["pool_step"], 1)
                pool.wait_ge(S["pool_step"], 5 * n)
                tt(rstd3[:, 64:96], rstd[:], zero32[:], add).then_inc(S["rstd_ready"], 1)

            def residual_input(t):
                pool.wait_ge(S["x_loaded"], 32 * t + 32)
                nc.gpsimd.tensor_tensor(xb[:], x_in[:], b_p[:, 0:1].broadcast_to([128, TOK]),
                                        ALU.add).then_inc(S["xb_ready"], 1)

            residual_input(0)
            root(1)
            with pool.Fori(0, PAIRS) as p:
                with pool.Fori(0, TILES) as i:
                    T = p * TILES + i
                    root(2 * T + 2)
                    pool.wait_ge(S["x1_ready"], 4 * T + 4)
                    residual_input(T + 1)
                    root(2 * T + 3)

        @block.tensor
        def _(pe):
            mm = nc.tensor.matmul
            pe.wait_ge(S["dve_prep"], 1)
            M = ps[:, 7, :]
            for s, h in halves():
                mm(ps[h, 0, 0:64], gain_w[h, 0:64], centre[h, 64 * s:64 * s + 64], start=True, stop=True)
                mm(ps[h, 0, 64:128], gain_w[h, 64:128], centre[h, 64 * s:64 * s + 64], start=True, stop=True)
                mm(ps[h, 0, 128:192], centre[h, 64 * s:64 * s + 64], gain_w[h, 128:192], start=True, stop=True)
                mm(ps[h, 1, 0:HID], centre[h, 64 * s:64 * s + 64], gain_1[h, :], start=True, stop=True)
                for k in range(3):
                    mm(ps[h, 2, k:k + 1], raw_w[h, 64 * k:64 * k + 64], cols[h, B1N:B1N + 1], start=True, stop=True)
            for k in range(HC):
                mm(ps[:, 3, k:k + 1], raw_1[0:64, 128 * k:128 * k + 128], cols[0:64, B2N:B2N + 1],
                   start=True, stop=True)
            for hp in range(2):
                last = nc.tensor.transpose(ps[:, 4, 64 * hp:64 * hp + 64],
                                           bias_t[0:64, 2 * hp:2 * hp + 2, :].rearrange("p h n -> p (h n)"),
                                           ident[0:64, 0:64])
            last.then_inc(S["prep_mm"], 1)
            pe.wait_ge(S["prep_ev"], 1)
            for s, h in halves():
                for hh in range(NH):
                    mm(ps[h, 0, 64 * hh:64 * hh + 64], q_masked[h, hh, :], qk_t[h, 64:128], start=True, stop=True)
                    mm(ps[h, 1, hh:hh + 1], qk_t[h, 64:128], vecs[h, 4 + hh:5 + hh], start=True, stop=True)
                last = mm(ps[h, 2, 0:1], raw_p[h, :], vecs[h, 2:3], start=True, stop=True)
            last.then_inc(S["prep_mm"], 1)
            pe.wait_ge(S["ready"], 1)

            def hi(ap):
                return ap.bitcast(BF16)[:, 1::2]

            def norm_mean(base, n, rhs, first=False):
                if n >= 2 or not first:
                    pe.wait_ge(S["ln_read"], base + n - 1)
                mm(ps[:, n % 2, :], mean_all[:], rhs, start=True, stop=True).then_inc(S["ln_mm"], 1)

            def norm_stats(n, c):
                pe.wait_ge(S["squared"], 4 * n - 3 + c)
                for k in range(4 * c, 4 * c + 4):
                    last = mm(ps[:, stat_bank, 2 * k:2 * k + 2], sq[:, 128 * k:128 * k + 128], mean_of[:],
                              start=True, stop=True)
                if c == NCH - 1:
                    last.then_inc(S["stats"], 1)

            def norm_turn(n):
                pe.wait_ge(S["rstd_ready"], n)
                nc.tensor.transpose(ps[0:96, stat_bank, 64:128].bitcast(BF16), rstd3[:],
                                    ident_bf[:]).then_inc(S["rstd_tp"], 1)

            def norm_spread(base, n, ln, k, first=False):
                pe.wait_ge(S["rstd_copied"], ln)
                if n >= 2 or not first:
                    pe.wait_ge(S["ln_read"], base + n - 1)
                bank = n % 2
                for j in range(4):
                    last = mm(ps[:, bank, 128 * j:128 * j + 128], pick_row[:, 4 * k + j, :], rstd_t[:],
                              start=True, stop=True)
                last.then_inc(S["ln_mm"], 1)

            x_windows = x_in[:].rearrange("p (r w c) -> p w r c", r=WS, c=WS)
            z1_flat = z1[:].rearrange("p w t -> p (w t)")

            def x_chunk(k):
                return x_windows[:, 8 * k:8 * k + 8, :, :]

            def x1_chunk(k):
                return x1[:, 2 + 2 * k:4 + 2 * k, 1:257]

            def project_u(g, k, hh):
                n = 4 * k + hh
                if n >= 2:
                    pe.wait_ge(S["u_ready"], 16 * g + n - 1)
                mm(ps[:, u_banks[n % 2], :], w_u[:, hh, :], z1_flat[:, BANK * k:BANK * k + BANK],
                   start=True, stop=True).then_inc(S["u_mm"], 1)
                if k:
                    guard(g, k - 1, hh)

            def project_v(g, k):
                pe.wait_ge(S["zbd_ready"], 4 * g + k + 1)
                if k:
                    pe.wait_ge(S["v_ready"], 4 * g + k)
                for w8 in range(8):
                    last = mm(ps[:, o_bank, 64 * w8:64 * w8 + 64], z_bd[:, 8 * k + w8, :], w_v[:],
                              start=True, stop=True)
                last.then_inc(S["v_mm"], 1)

            def guard(g, k, j):
                n = 4 * k + j
                hp, w4 = j // 2, j % 2
                pe.wait_ge(S["u_ready"], 16 * g + 4 * k + 2 * hp + 2)
                if n >= 2:
                    pe.wait_ge(S["guard_max"], 16 * g + n - 1)
                bank = s_bank + n % 2
                mm(ps[:, bank, :], ident_bf[:], bias_g[:, hp:hp + 1, :].broadcast_to([128, 8, 64]),
                   start=True, stop=False, skip_group_check=True)
                for q in range(4):
                    w = 8 * k + 4 * w4 + q
                    last = mm(ps[:, bank, 128 * q:128 * q + 128],
                              hi(u[:, w, 2 * hp:2 * hp + 2, :].rearrange("p a n -> p (a n)")),
                              hi(z_bd[:, w, :]), start=False, stop=(q == 3), skip_group_check=True)
                last.then_inc(S["guard_mm"], 1)

            def max_turn(g, ln):
                pe.wait_ge(S["rstd_copied"], ln)
                pe.wait_ge(S["guard_max"], 16 * g + 16)
                nc.tensor.transpose(ps[:, stat_bank, 128:192].bitcast(BF16), mx[:], ident_bf[:]).then_inc(S["max_tp"], 1)

            def rounds(T):
                def scores(r):
                    bank = s_bank + r % 2
                    if r >= 2:
                        pe.wait_ge(S["exp_done"], 16 * T + r - 1)
                    mm(ps[:, bank, :], twice[:], bias_s[:].rearrange("p h n -> p (h n)").unsqueeze(1).broadcast_to(
                        [128, 2, 256]), start=True, stop=False, skip_group_check=True)
                    for w2 in range(2):
                        w = 2 * r + w2
                        for hp in range(2):
                            mm(ps[:, bank, 256 * w2 + 128 * hp:256 * w2 + 128 * hp + 128],
                               pick_max[:, w // 8, hp, w % 8, :], mx_t[:], start=False, stop=False,
                               skip_group_check=True)
                        last = mm(ps[:, bank, 256 * w2:256 * w2 + 256], z_bd[:, w, :],
                                  u[:, w, :, :].rearrange("p h n -> p (h n)"), start=False,
                                  stop=True, skip_group_check=True)
                    last.then_inc(S["score_mm"], 1)

                def values(r):
                    pe.wait_ge(S["exp_done"], 16 * T + r + 1)
                    if r:
                        pe.wait_ge(S["o_ready"], 32 * T + 2 * r)
                    for w2 in range(2):
                        for hp in range(2):
                            c = 66 * (2 * w2 + hp)
                            last = mm(ps[:, o_bank, c:c + 66],
                                      prob[:, r % 4, 256 * w2 + 128 * hp:256 * w2 + 128 * hp + 128],
                                      v[:, 2 * r + w2, hp, :, :].rearrange("p s d -> p (s d)"), start=True, stop=True)
                    last.then_inc(S["pv_mm"], 1)

                def turn(r):
                    pe.wait_ge(S["o_ready"], 32 * T + 2 * r + 2)
                    if r % 4 == 0 and r:
                        pe.wait_ge(S["o_copied"], 4 * T + r // 4)
                    nc.tensor.transpose(ps[:, t_bank, 128 * (r % 4):128 * (r % 4) + 128], o_n[:, r % 2, :],
                                        ident[:]).then_inc(S["o_tp"], 1)

                def project(q):
                    pe.wait_ge(S["o_copied"], 4 * T + q + 1)
                    if q:
                        pe.wait_ge(S["x1_ready"], 4 * T + q)
                    for w2 in range(2):
                        for h2 in range(2):
                            last = mm(ps[:, proj_bank, 256 * w2:256 * w2 + 256], w_p[:, w2, h2, :],
                                      o_t[:, :, 64 * h2:64 * h2 + 64], start=(h2 == 0), stop=(h2 == 1))
                    last.then_inc(S["proj_mm"], 1)

                pe.wait_ge(S["f_ready"], 4 * T + 1)
                for r in range(ROUNDS + 3):
                    if r < ROUNDS:
                        scores(r)
                    if r == 1:
                        pe.wait_ge(S["x_loaded"], 32 * T + 64)
                    if r in (1, 3, 5, 7):
                        norm_mean(8 + 16 * T, r // 2, x_chunk(r // 2))
                    if r in (4, 6, 8, 10):
                        norm_stats(2 * T + 2, r // 2 - 2)
                    if r == ROUNDS:
                        norm_turn(2 * T + 2)
                    if 1 <= r <= ROUNDS:
                        values(r - 1)
                    if 2 <= r <= ROUNDS + 1:
                        turn(r - 2)
                    if r == ROUNDS + 1:
                        norm_spread(8 + 16 * T, 4, 2 * T + 2, 0)
                        norm_spread(8 + 16 * T, 5, 2 * T + 2, 1)
                    if r >= 6 and (r - 6) % 4 == 0:
                        project((r - 6) // 4)

            def up(T, k):
                pe.wait_ge(S["ln_read"], 16 * T + 21 + k)
                for s, h in halves():
                    for hc in range(HC):
                        j = 2 * s + hc
                        if k:
                            pe.wait_ge(S["gelu_done"], 16 * T + 4 * (k - 1) + j + 1)
                        mm(ps[:, f_banks[j], :], w_1[h, 128 * hc:128 * hc + 128], z2[h, BANK * k:BANK * k + BANK],
                           start=True, stop=True).then_inc(S["f1_mm"], 1)

            def down(T, k):
                if k >= 2:
                    pe.wait_ge(S["f_ready"], 4 * T + k)
                for s, h in halves():
                    for hc in range(HC):
                        j = 2 * s + hc
                        pe.wait_ge(S["gelu_done"], 16 * T + 4 * k + j + 1)
                        last = mm(ps[h, s_bank + k % 2, :], w_2[:, hc, :], hid[:, k % 2, j, :],
                                  start=(hc == 0), stop=(hc == HC - 1))
                last.then_inc(S["f2_mm"], 1)

            pe.wait_ge(S["x_loaded"], 32)
            for k in range(4):
                norm_mean(0, k, x_chunk(k), first=True)
            for k in range(4):
                norm_stats(1, k)
            norm_turn(1)
            for k in range(4):
                norm_spread(0, 4 + k, 1, k)
                pe.wait_ge(S["ln_read"], 5 + k)
                for hh in range(NH):
                    project_u(0, k, hh)
                project_v(0, k)
            for j in range(4):
                guard(0, 3, j)
            max_turn(0, 1)

            with pe.Fori(0, PAIRS) as p:
                with pe.Fori(0, TILES) as i:
                    T = p * TILES + i
                    g = T + 1

                    X = 8 + 16 * T

                    pe.wait_ge(S["max_copied"], T + 1)
                    rounds(T)
                    pe.wait_ge(S["ln_read"], 16 * T + 13)
                    for hh in range(NH):
                        if hh == 1:
                            pe.wait_ge(S["x1_ready"], 4 * T + 4)
                        project_u(g, 0, hh)
                    project_v(g, 0)
                    norm_mean(X, 6, x1_chunk(0))
                    norm_mean(X, 7, x1_chunk(1))
                    pe.wait_ge(S["ln_read"], 16 * T + 14)
                    project_u(g, 1, 0)
                    project_u(g, 1, 1)
                    norm_spread(X, 8, 2 * T + 2, 2)
                    project_u(g, 1, 2)
                    project_u(g, 1, 3)
                    project_v(g, 1)
                    norm_mean(X, 9, x1_chunk(2))
                    norm_stats(2 * T + 3, 0)
                    norm_stats(2 * T + 3, 1)
                    norm_mean(X, 10, x1_chunk(3))
                    pe.wait_ge(S["ln_read"], 16 * T + 17)
                    project_u(g, 2, 0)
                    project_u(g, 2, 1)
                    norm_spread(X, 11, 2 * T + 2, 3)
                    project_u(g, 2, 2)
                    project_u(g, 2, 3)
                    project_v(g, 2)
                    norm_stats(2 * T + 3, 2)
                    norm_stats(2 * T + 3, 3)
                    pe.wait_ge(S["ln_read"], 16 * T + 20)
                    for hh in range(NH):
                        project_u(g, 3, hh)
                    project_v(g, 3)
                    for j in range(4):
                        guard(g, 3, j)
                    norm_turn(2 * T + 3)
                    max_turn(g, 2 * T + 3)
                    pe.wait_ge(S["v_ready"], 4 * g + 4)
                    norm_spread(X, 12, 2 * T + 3, 0)
                    norm_spread(X, 13, 2 * T + 3, 1)
                    pe.wait_ge(S["max_copied"], g + 1)
                    up(T, 0)
                    norm_spread(X, 14, 2 * T + 3, 2)
                    up(T, 1)
                    norm_spread(X, 15, 2 * T + 3, 3)
                    down(T, 0)
                    up(T, 2)
                    down(T, 1)
                    up(T, 3)
                    down(T, 2)
                    down(T, 3)
                pe.wait_ge(S["flush_done"], p + 1)
                mm(ps[0:G * K2, m_bank, 0:2], conv_w_t[:], mean2[:], start=True, stop=True).then_inc(S["lf_mm"], 1)
                pe.wait_ge(S["lf_dve"], 2 * p + 2)
                for s, h in halves():
                    last = mm(ps[h, m_bank, 64:64 + K2], gsel[:], lf_k[:, s, :], start=True, stop=True)
                last.then_inc(S["lf_mm"], 1)
                pe.wait_ge(S["phase2_ready"], p + 1)

        @block.scalar
        def _(act):
            actf = nc.scalar.activation

            def store_y(p, i, rows, r0=0):
                for s, h in halves():
                    act.dma_start(y_dram[p + PAIRS * s, :, bass.ds(i * WS, rows), :],
                                  f[h, r0:r0 + rows, :]).then_inc(S["y_stored"], 16)

            act.wait_ge(S["ready"], 1)

            def square(k, d, read):
                act.wait_ge(S["ln_read"], read)
                actf(sq[:, BANK * k:BANK * k + BANK], d[:, BANK * k:BANK * k + BANK], ACT.Square).then_inc(
                    S["squared"], 1)

            def copy_rstd(n):
                act.wait_ge(S["rstd_tp"], n)
                actf(rstd_t[:], ps[0:96, stat_bank, 64:128].bitcast(BF16), ACT.Copy).then_inc(S["rstd_copied"], 1)

            z1_flat = z1[:].rearrange("p w t -> p (w t)")

            def diagonal(k, read):
                act.wait_ge(S["ln_read"], read)
                for s, h in halves():
                    last = actf(z_bd[h, 8 * k:8 * k + 8, 64 * s:64 * s + 64], z1[h, 8 * k:8 * k + 8, :], ACT.Copy)
                last.then_inc(S["zbd_ready"], 1)

            def take_uv(g, k, read, beside=None):
                for hh in range(NH):
                    n = 4 * k + hh
                    act.wait_ge(S["u_mm"], 16 * g + n + 1)
                    actf(u[:, 8 * k:8 * k + 8, hh, :], ps[:, u_banks[n % 2], :].rearrange("p (w n) -> p w n", w=8),
                         ACT.Identity, bias=b_u[:, hh:hh + 1]).then_inc(S["u_ready"], 1)
                    if hh == 0:
                        diagonal(k, read)
                    if beside:
                        beside(k, hh)
                act.wait_ge(S["v_mm"], 4 * g + k + 1)
                for s, h in halves():
                    last = actf(v[h, 8 * k:8 * k + 8, :, s, 0:32],
                                ps[h, o_bank, :].rearrange("p (w a d) -> p w a d", w=8, a=2), ACT.Copy)
                last.then_inc(S["v_ready"], 1)

            def copy_max(g):
                act.wait_ge(S["max_tp"], g + 1)
                actf(mx_t[:], ps[:, stat_bank, 128:192].bitcast(BF16), ACT.Copy).then_inc(S["max_copied"], 1)

            for k in range(4):
                square(k, z1_flat, k + 1)
            copy_rstd(1)
            for k in range(4):
                take_uv(0, k, 5 + k)
            copy_max(0)

            def body(T, p, i, second):
                g = T + 1

                def copy_o(q):
                    act.wait_ge(S["o_tp"], 16 * T + 4 * q + 4)
                    if q:
                        act.wait_ge(S["proj_mm"], 4 * T + q)
                    actf(o_t[:, :, :].rearrange("p a b -> p (a b)"), ps[:, t_bank, :],
                         ACT.Copy).then_inc(S["o_copied"], 1)

                for r in range(ROUNDS):
                    act.wait_ge(S["score_mm"], 16 * T + r + 1)
                    if r >= 4:
                        act.wait_ge(S["pv_mm"], 16 * T + r - 3)
                    actf(prob[:, r % 4, :], ps[:, s_bank + r % 2, :], ACT.Exp).then_inc(S["exp_done"], 1)
                    if r >= 6 and (r - 6) % 4 == 0:
                        copy_o((r - 6) // 4)
                    if r in (3, 5, 7, 9):
                        square((r - 3) // 2, z1_flat, 16 * T + 9 + (r - 3) // 2)
                    if r == 11:
                        act.wait_ge(S["conv_step"], CONV_STEPS * T + 8)
                        actf(f[:, 0, :], f[:, 0, :], ACT.Identity, bias=b_y[:, 0:1], accum_out=acc[:, 0:1])
                    if r == 12:
                        actf(f[:, 1:WS, :], f[:, 1:WS, :], ACT.Identity, bias=b_y[:, 0:1],
                             accum_out=acc[:, 1:2]).then_inc(S["y_done"], 1)
                    if r == 14:
                        act.wait_ge(S["y_done"], T + 1)
                        store_y(p, i, WS)
                copy_rstd(2 * T + 2)
                copy_o(3)

                def beside(k, hh):
                    if (k, hh) == (0, 1):
                        act.wait_ge(S["y_stored"], 32 * (T + 2 * p + 1))
                        actf(f[:, 0, :], f[:, WS, :], ACT.Copy).then_inc(S["f_shift"], 1)
                    if (k, hh) == (0, 3):
                        act.wait_ge(S["x1_ready"], 4 * T + 4)
                        actf(f[:, 1:5, :], x1[:, 2:6, 1:257], ACT.Copy, scale=taps0[:, 4:5]).then_inc(
                            S["f_centre"], 1)
                    if (k, hh) == (1, 3):
                        act.wait_ge(S["f_shift"], T + 1)
                        actf(f[:, 5:9, :], x1[:, 6:10, 1:257], ACT.Copy, scale=taps0[:, 4:5]).then_inc(
                            S["f_centre"], 1)
                    if k in (1, 2) and hh in (1, 2):
                        c = 2 * (k - 1) + hh - 1
                        square(c, z2, 16 * T + (15, 16, 18, 19)[c])
                    if second and (k, hh) == (3, 1):
                        act.wait_ge(S["y_loaded"], 32 * (T - TILES) + 32)
                        actf(res[:], y_in[:, 1:9, 1:257], ACT.Identity, bias=const1[:, 0:1],
                             scale=taps1[:, 4:5]).then_inc(S["tap_first"], 1)

                for k in range(NCH):
                    take_uv(g, k, 16 * T + (13, 14, 17, 20)[k], beside)
                copy_rstd(2 * T + 3)
                copy_max(g)
                for k in range(NCH):
                    for j in range(4):
                        act.wait_ge(S["f1_mm"], 16 * T + 4 * k + j + 1)
                        if k >= 2 and j == 0:
                            act.wait_ge(S["f2_mm"], 4 * T + k - 1)
                        actf(hid[:, k % 2, j, :], ps[:, f_banks[j], :], ACT.Gelu,
                             bias=b_1[:, j % HC:j % HC + 1]).then_inc(S["gelu_done"], 1)

            def flush(p):
                act.wait_ge(S["flush_step"], 2 * p + 1)
                actf(f[:, 0, :], f[:, 0, :], ACT.Identity, bias=b_y[:, 0:1], accum_out=acc[:, 0:1])
                actf(f[:, 1:WS, :], f[:, 1:WS, :], ACT.Identity, bias=b_y[:, 0:1],
                     accum_out=acc[:, 1:2]).then_inc(S["lf_act"], 1)
                act.wait_ge(S["lf_act"], 3 * p + 1)
                store_y(p, TILES, WS)
                act.wait_ge(S["flush_step"], 2 * p + 2)
                actf(f[:, WS, :], f[:, WS, :], ACT.Identity, bias=b_y[:, 0:1],
                     accum_out=acc[:, 0:1]).then_inc(S["lf_act"], 1)
                act.wait_ge(S["lf_act"], 3 * p + 2)
                store_y(p, TILES + 1, 1, WS)
                act.wait_ge(S["lf_dve"], 2 * p + 1)
                actf(lf[:], lf[:], ACT.Tanh).then_inc(S["lf_act"], 1)

            with act.Fori(0, TILES) as i:
                body(i, 0, i, False)
            flush(0)
            with act.Fori(1, PAIRS) as p:
                with act.Fori(0, TILES) as i:
                    body(p * TILES + i, p, i, True)
                flush(p)
            act.wait_ge(S["phase2_ready"], PAIRS)
            with act.Fori(0, TILES // 2) as j:
                for n in range(2):
                    act.wait_ge(S[f"e_loaded{n}"], 32 * j + 32)
                    actf(res_end[:, n, :, :], y_end[:, n, 1:9, 1:257], ACT.Identity, bias=const1[:, 0:1],
                         scale=taps1[:, 4:5]).then_inc(S[f"e_first{n}"], 1)
                for n in range(2):
                    act.wait_ge(S[f"e_done{n}"], j + 1)
                    for s, h in halves():
                        act.dma_start(out[PAIRS - 1 + PAIRS * s, :, bass.ds((2 * j + n) * WS, WS), :],
                                      res_end[h, n, :, :]).then_inc(S[f"e_stored{n}"], 16)
                for n in range(2):
                    act.wait_ge(S[f"e_stored{n}"], 32 * j + 32)

        @block.vector
        def _(dve):
            V = nc.vector
            step = [0]

            def chain(ins):
                step[0] += 1
                ins.then_inc(S["dve_chain"], 1)
                dve.wait_ge(S["dve_chain"], step[0])

            chain(V.memset(w_p[:].rearrange("p a b c -> p (a b c)"), 0.0))
            V.memset(w_u[:].rearrange("p a b -> p (a b)"), 0.0).then_inc(S["z_init"], 1)
            chain(V.memset(x1[:].rearrange("p a b -> p (a b)"), 0.0))
            chain(V.memset(v[:].rearrange("p w a s d -> p (w a s d)"), 0.0))
            for s, h in halves():
                chain(V.memset(v[h, :, :, s, 32:33], 1.0))
            chain(V.memset(z_bd[:].rearrange("p w t -> p (w t)"), 0.0))
            chain(V.memset(f[:].rearrange("p a b -> p (a b)"), 0.0))
            dve.wait_ge(S["const_loaded"], n_const[0])
            chain(V.tensor_copy(ident_bf[:], ident[:]))
            for j in range(3):
                chain(V.tensor_copy(pick_row[32 * j:32 * j + 32, :, :].rearrange("r k (s c) -> r (k s) c", s=2),
                                    ident[32 * j:32 * j + 32, 32 * j:32 * j + 32].unsqueeze(2).broadcast_to([32, 32, 64])))
            chain(V.tensor_scalar(mean_all[:].rearrange("p (s c) -> p s c", s=2),
                                  mean_of[:].unsqueeze(2).broadcast_to([128, 2, 64]), 1.0, None, ALU.mult))
            for s, h in halves():
                chain(V.tensor_scalar(twice[h, :].rearrange("p (a m) -> p a m", a=2),
                                      ident[h, 64 * s:64 * s + 64].unsqueeze(1).broadcast_to([64, 2, 64]),
                                      1.0 if s == 0 else 2.0 ** -11, None, ALU.mult))
            for k in range(NCH):
                for hp in range(2):
                    for s in range(2):
                        i0 = 32 * k + 16 * hp + s
                        V.tensor_scalar(pick_max[:, k, hp, :, 64 * s:64 * s + 64],
                                        ident[:, i0:i0 + 15:2].unsqueeze(2).broadcast_to([128, 8, 64]),
                                        -1.0, None, ALU.mult)
            rest = sq[:, 0:256].rearrange("p (h n) -> p h n", h=NH)
            chain(V.tensor_copy(bias_s[:], bias_t[:]))
            chain(V.tensor_tensor(rest, bias_t[:], bias_s[:], ALU.subtract))
            chain(V.tensor_scalar(bias_s[64:128, :, :], rest[64:128, :, :], 2.0 ** 11, None, ALU.mult))
            chain(V.tensor_scalar(gain_w[:], raw_w[:], cols[:, G1:G1 + 1], None, ALU.mult))
            V.tensor_scalar(gain_1[:], raw_1[:], cols[:, G2:G2 + 1], None, ALU.mult).then_inc(S["dve_prep"], 1)
            dve.wait_ge(S["prep_mm"], 1)
            chain(V.tensor_copy(qk_t[:], ps[:, 0, 0:128]))
            chain(V.tensor_copy(w_v[:], ps[:, 0, 128:192]))
            chain(V.tensor_copy(w_1[:], ps[:, 1, 0:HID]))
            chain(V.tensor_tensor(vecs[:, 0:1], ps[:, 2, 0:1], cols[:, QB:QB + 1], ALU.add))
            chain(V.tensor_tensor(vecs[:, 2:3], ps[:, 2, 2:3], cols[:, VB:VB + 1], ALU.add))
            chain(V.tensor_tensor(b_1[:], b_1[:], ps[:, 3, 0:HC], ALU.add))
            chain(V.tensor_copy(bias_g[:], ps[:, 4, 0:128].rearrange("p (a m) -> p a m", a=2)))
            for hh in range(NH):
                chain(V.tensor_scalar(q_masked[:, hh, :], qk_t[:, 0:64], headmask[:, hh:hh + 1], None, ALU.mult))
            chain(V.tensor_scalar(vecs[:, 4:8], headmask[:], vecs[:, 0:1], None, ALU.mult))
            V.memset(vecs[:, 8:9], 0.0).then_inc(S["prep_ev"], 1)
            dve.wait_ge(S["prep_mm"], 2)
            for s, h in halves():
                chain(V.tensor_copy(w_u[h, :, 64 * s:64 * s + 64],
                                    ps[h, 0, 0:256].rearrange("p (h c) -> p h c", h=NH)))
            chain(V.tensor_copy(b_u[:], ps[:, 1, 0:NH]))
            chain(V.tensor_tensor(b_p[:], ps[:, 2, 0:1], cols[:, PB:PB + 1], ALU.add))
            chain(V.tensor_tensor(b_y[:], cols[:, FB:FB + 1], cols[:, DB:DB + 1], ALU.add))
            chain(V.tensor_scalar(taps0[:, 4:5], taps0[:, 4:5], 1.0, None, ALU.add))
            chain(V.scalar_tensor_tensor(l1c[:, 3:4], l1c[:, 2:3], 1.0, l1c[:, 0:1], ALU.add, ALU.mult))
            chain(V.tensor_scalar(l1c[:, 4:5], l1c[:, 1:2], 1.0, None, ALU.add))
            chain(V.scalar_tensor_tensor(l1c[:, 5:6], l1c[:, 2:3], -1.0, l1c[:, 0:1], ALU.mult, ALU.mult))
            V.tensor_scalar(bn[:, 6:7], bn[:, 3:4], BN_EPS, None, ALU.add).then_inc(S["bn_var"], 1)
            V.memset(tot[:], 0.0).then_inc(S["f_ready"], 1)
            chain(V.memset(flags[:], 0.0))
            dve.wait_ge(S["bn_root"], 1)
            chain(V.tensor_tensor(bn[:, 4:5], bn[:, 0:1], bn[:, 7:8], ALU.mult))
            chain(V.tensor_tensor(bn[:, 6:7], bn[:, 2:3], bn[:, 4:5], ALU.mult))
            chain(V.tensor_tensor(bn[:, 5:6], bn[:, 1:2], bn[:, 6:7], ALU.subtract))
            V.memset(acc[:], 0.0).then_inc(S["ready"], 1)

            def d1(n, k):
                dve.wait_ge(S["ln_mm"], n)
                xp = x_in[:].rearrange("p (r w c) -> p w r c", r=WS, c=WS)[:, 8 * k:8 * k + 8, :, :]
                V.tensor_tensor(z1[:, 8 * k:8 * k + 8, :].rearrange("p w (r c) -> p w r c", c=WS), xp,
                                ps[:, k % 2, :].rearrange("p (w r c) -> p w r c", w=8, c=WS),
                                ALU.subtract).then_inc(S["ln_read"], 1)

            def variance(n):
                dve.wait_ge(S["stats"], n)
                V.tensor_scalar(var[:], ps[:, stat_bank, 0:32], LN_EPS, None, ALU.add).then_inc(S["var_ready"], 1)

            def apply1(n, bank, k):
                dve.wait_ge(S["ln_mm"], n)
                zk = z1[:, 8 * k:8 * k + 8, :].rearrange("p w t -> p (w t)")
                V.tensor_tensor(zk, zk, ps[:, bank, :], ALU.mult).then_inc(S["ln_read"], 1)

            def row_max(g, k, j):
                n = 4 * k + j
                dve.wait_ge(S["guard_mm"], 16 * g + n + 1)
                V.tensor_reduce(mx[:, 8 * n:8 * n + 8], ps[:, s_bank + n % 2, :].rearrange("p (w m) -> p w m", w=8),
                                AX.X, ALU.max).then_inc(S["guard_max"], 1)

            def residual(T, q):
                dve.wait_ge(S["proj_mm"], 4 * T + q + 1)
                dve.wait_ge(S["xb_ready"], T + 1)
                for w2 in range(2):
                    w0 = 8 * q + w2
                    last = V.tensor_tensor(
                        x1[:, 2:10, 1:257].rearrange("p r (w c) -> p w r c", c=WS)[:, w0:w0 + 7:2, :, :],
                        ps[:, proj_bank, 256 * w2:256 * w2 + 256].rearrange("p (w r c) -> p w r c", w=4, r=WS),
                        xb[:].rearrange("p (r w c) -> p w r c", r=WS, c=WS)[:, w0:w0 + 7:2, :, :],
                        ALU.add)
                last.then_inc(S["x1_ready"], 1)

            TAPS = [t for t in range(K2) if t != 4]

            def conv_tap(n, rows, src, dst, wait):
                t = TAPS[n]
                return V.scalar_tensor_tensor(dst, src[:, t // 3:t // 3 + rows, t % 3:t % 3 + IMG],
                                              wait[:, t:t + 1], dst, ALU.mult, ALU.add)

            dve.wait_ge(S["x_loaded"], 32)
            for k in range(4):
                d1(k + 1, k)
            variance(1)
            for k in range(4):
                apply1(5 + k, k % 2, k)
                if k:
                    for j in range(4):
                        row_max(0, k - 1, j)
            for j in range(4):
                row_max(0, 3, j)

            def body(T, second):
                g = T + 1
                X = 8 + 16 * T
                N = T - TILES

                def d2(n, k):
                    dve.wait_ge(S["ln_mm"], X + n + 1)
                    V.tensor_tensor(z2[:, BANK * k:BANK * k + BANK].rearrange("p (r w) -> p r w", r=2),
                                    x1[:, 2 + 2 * k:4 + 2 * k, 1:257],
                                    ps[:, n % 2, :].rearrange("p (r w) -> p r w", r=2),
                                    ALU.subtract).then_inc(S["ln_read"], 1)

                def apply2(n, k):
                    dve.wait_ge(S["ln_mm"], X + n + 1)
                    zk = z2[:, BANK * k:BANK * k + BANK]
                    V.tensor_tensor(zk, zk, ps[:, n % 2, :], ALU.mult).then_inc(S["ln_read"], 1)

                def conv_half(m, before, known=False):
                    if not known:
                        dve.wait_ge(S["conv_step"], before - 1)
                    r0 = HALF * (m % 2)
                    conv_tap(m // 2, HALF, x1[:, r0:r0 + HALF + 2, :], f[:, r0:r0 + HALF, :], taps0).then_inc(
                        S["conv_step"], 1)

                def second_half(m):
                    if m == 0:
                        dve.wait_ge(S["tap_first"], N + 1)
                        dve.wait_ge(S["edge_done"], N + 1)
                    elif m > 1:
                        dve.wait_ge(S["tap_step"], 15 * N + m - (m < 15))
                    r0 = HALF * (m % 2)
                    conv_tap(m // 2, HALF, y_in[:, r0:r0 + HALF + 2, :], res[:, r0:r0 + HALF, :], taps1).then_inc(
                        S["tap_step" if m < 15 else "res_done"], 1)

                for r in range(ROUNDS):
                    if r in (2, 4, 6, 8):
                        if r == 2:
                            dve.wait_ge(S["x_loaded"], 32 * T + 64)
                        d1(X + r // 2, r // 2 - 1)
                    dve.wait_ge(S["pv_mm"], 16 * T + r + 1)
                    O = ps[:, o_bank, 0:264].rearrange("p (g d) -> p g d", d=33)
                    V.reciprocal(rsum[:, r % 2, :], O[:, :, 32:33].rearrange("p g o -> p (g o)")).then_inc(
                        S["o_recip"], 1)
                    dve.wait_ge(S["o_recip"], 16 * T + r + 1)
                    if r >= 2:
                        dve.wait_ge(S["o_tp"], 16 * T + r - 1)
                    for h2, h in halves():
                        V.tensor_tensor(o_n[h, r % 2, :].rearrange("p (g d) -> p g d", d=HD),
                                        O[h, :, 16 * h2:16 * h2 + 16],
                                        rsum[h, r % 2, :].unsqueeze(2).broadcast_to([64, 8, HD]),
                                        ALU.mult).then_inc(S["o_ready"], 1)
                    if r < 8:
                        conv_half(8 + r, CONV_STEPS * T + r, known=r < 2)
                    if r == 8:
                        dve.wait_ge(S["conv_step"], CONV_STEPS * T + 8)
                        V.tensor_copy(x1[:, 0:2, :], x1[:, 8:10, :]).then_inc(S["conv_step"], 1)
                        dve.wait_ge(S["conv_step"], CONV_STEPS * T + 9)
                    if r in (9, 12, 15):
                        residual(T, (r - 9) // 3)
                    if r == 11:
                        variance(2 * T + 2)
                apply1(X + 5, 0, 0)
                apply1(X + 6, 1, 1)
                residual(T, 3)
                dve.wait_ge(S["x1_ready"], 4 * T + 4)
                d2(6, 0)
                d2(7, 1)
                row_max(g, 0, 0)
                row_max(g, 0, 1)
                apply1(X + 9, 0, 2)
                row_max(g, 0, 2)
                row_max(g, 0, 3)
                d2(9, 2)
                d2(10, 3)
                row_max(g, 1, 0)
                row_max(g, 1, 1)
                apply1(X + 12, 1, 3)
                done = CONV_STEPS * T + 9
                dve.wait_ge(S["f_shift"], T + 1)
                dve.wait_ge(S["f_centre"], 2 * T + 2)
                conv_half(0, done)
                conv_half(1, done + 1)
                row_max(g, 1, 2)
                conv_half(2, done + 2)
                row_max(g, 1, 3)
                conv_half(3, done + 3)
                variance(2 * T + 3)
                for j in range(4):
                    row_max(g, 2, j)
                    conv_half(4 + j, done + 4 + j)
                for j in range(4):
                    row_max(g, 3, j)
                if second:
                    dve.wait_ge(S["y_loaded"], 32 * N + 32)
                    V.tensor_copy(y_in[:, :, 0:1], y_in[:, :, 2:3])
                    V.tensor_copy(y_in[:, :, 257:258], y_in[:, :, 255:256]).then_inc(S["edge_done"], 1)
                dve.wait_ge(S["y_done"], T + 1)
                V.scalar_tensor_tensor(tot[:], acc[:, 0:1], flags[:, 0:1], tot[:], ALU.mult, ALU.add).then_inc(
                    S["tot_step"], 1)
                dve.wait_ge(S["tot_step"], 4 * T + 1)
                V.scalar_tensor_tensor(tot[:], acc[:, 1:2], flags[:, 1:2], tot[:], ALU.mult, ALU.add).then_inc(
                    S["tot_step"], 1)
                V.tensor_copy(flags[:, 0:1], flags[:, 1:2]).then_inc(S["tot_step"], 1)
                dve.wait_ge(S["tot_step"], 4 * T + 3)
                V.memset(flags[:, 1:2], 1.0).then_inc(S["tot_step"], 1)
                m2 = 0
                for k in range(NCH):
                    apply2(12 + k, k)
                    if second and k:
                        second_half(m2)
                        second_half(m2 + 1)
                        m2 += 2
                dve.wait_ge(S["conv_step"], CONV_STEPS * T + CONV_STEPS)
                dve.wait_ge(S["tot_step"], 4 * T + 4)
                for k in range(NCH):
                    dve.wait_ge(S["f2_mm"], 4 * T + k + 1)
                    fk = f[:, 1 + 2 * k:3 + 2 * k, :]
                    V.tensor_tensor(fk, fk, ps[:, s_bank + k % 2, :].rearrange("p (r w) -> p r w", r=2),
                                    ALU.add).then_inc(S["f_ready"], 1)
                    if second and k < 3:
                        for _ in range(4 if k < 2 else 2):
                            second_half(m2)
                            m2 += 1
                dve.wait_ge(S["f_ready"], 4 * T + 5)

            def finish(p):
                n_fl = [0]

                def flush(ins):
                    n_fl[0] += 1
                    ins.then_inc(S["flush_chain"], 1)
                    dve.wait_ge(S["flush_chain"], FLUSH_STEPS * p + n_fl[0])

                dve.wait_ge(S["f_ready"], 4 * TILES * (p + 1) + 1)
                for n in range(4, 7):
                    flush(conv_tap(n, WS, x1, f[:, 0:WS, :], taps0))
                conv_tap(7, WS, x1, f[:, 0:WS, :], taps0).then_inc(S["flush_step"], 1)
                flush(V.tensor_copy(x1[:, 0:2, :], x1[:, 8:10, :]))
                flush(V.memset(x1[:, 2, :], 0.0))
                for n in range(7):
                    flush(conv_tap(n, 1, x1, f[:, WS:WS + 1, :], taps0))
                dve.wait_ge(S["lf_act"], 3 * p + 1)
                flush(V.tensor_tensor(tot[:], tot[:], acc[:, 0:1], ALU.add))
                flush(V.tensor_tensor(tot[:], tot[:], acc[:, 1:2], ALU.add))
                conv_tap(7, 1, x1, f[:, WS:WS + 1, :], taps0).then_inc(S["flush_step"], 1)
                dve.wait_ge(S["lf_act"], 3 * p + 2)
                flush(V.tensor_tensor(tot[:], tot[:], acc[:, 0:1], ALU.add))
                flush(V.tensor_scalar(tot[:], tot[:], 1.0 / (IMG * IMG), None, ALU.mult))
                V.tensor_scalar(mean2[:], mean_of[:], tot[:, 0:1], float(C), ALU.mult, ALU.mult).then_inc(
                    S["flush_done"], 1)
                dve.wait_ge(S["lf_mm"], 2 * p + 1)
                V.tensor_scalar(lf[:], ps[0:G * K2, m_bank, 0:2], bn[:, 4:5], bn[:, 5:6], ALU.mult,
                                ALU.add).then_inc(S["lf_dve"], 1)
                dve.wait_ge(S["lf_act"], 3 * p + 3)
                V.tensor_scalar(lf_k[:, 0, :], kmask[:], lf[:, 0:1], None, ALU.mult)
                V.tensor_scalar(lf_k[:, 1, :], kmask[:], lf[:, 1:2], None, ALU.mult).then_inc(S["lf_dve"], 1)
                dve.wait_ge(S["lf_mm"], 2 * p + 2)
                flush(V.tensor_scalar(taps1[:], ps[:, m_bank, 64:64 + K2], l1c[:, 3:4], None, ALU.mult))
                flush(V.tensor_tensor(taps1[:, 4:5], taps1[:, 4:5], l1c[:, 4:5], ALU.add))
                flush(V.tensor_tensor(const1[:], tot[:], l1c[:, 5:6], ALU.mult))
                flush(V.memset(tot[:], 0.0))
                flush(V.memset(flags[:], 0.0))
                dve.wait_ge(S["y_stored"], 32 * (TILES + 2) * (p + 1))
                flush(V.memset(f[:].rearrange("p a b -> p (a b)"), 0.0))
                V.memset(x1[:].rearrange("p a b -> p (a b)"), 0.0).then_inc(S["phase2_ready"], 1)
                assert n_fl[0] == FLUSH_STEPS

            with dve.Fori(0, TILES) as i:
                body(i, False)
            finish(0)
            with dve.Fori(1, PAIRS) as p:
                with dve.Fori(0, TILES) as i:
                    body(p * TILES + i, True)
                finish(p)
            with dve.Fori(0, TILES // 2) as j:
                for n in range(2):
                    dve.wait_ge(S[f"e_loaded{n}"], 32 * j + 32)
                    V.tensor_copy(y_end[:, n, :, 0:1], y_end[:, n, :, 2:3])
                    V.tensor_copy(y_end[:, n, :, 257:258], y_end[:, n, :, 255:256]).then_inc(S[f"e_edge{n}"], 1)
                    dve.wait_ge(S[f"e_edge{n}"], j + 1)
                    dve.wait_ge(S[f"e_first{n}"], j + 1)
                    for k in range(8):
                        ins = conv_tap(k, WS, y_end[:, n, :, :], res_end[:, n, :, :], taps1)
                        if k < 7:
                            ins.then_inc(S[f"e_step{n}"], 1)
                            dve.wait_ge(S[f"e_step{n}"], 7 * j + k + 1)
                        else:
                            ins.then_inc(S[f"e_done{n}"], 1)


_INS = ["qkv_w", "proj_w", "ffn_w1", "ffn_w2", "qkv_b", "proj_b", "norm1_g", "norm1_b", "norm2_g", "norm2_b",
        "ffn_b1", "ffn_w2_b", "dw_w", "dw_b"]
_INS1 = ["conv_w", "bn_gamma", "bn_beta", "bn_mean", "bn_var", "lamb_l", "lamb_h", "inside_all"]


def constants():
    import numpy as np
    f = np.float32
    two = np.kron(np.eye(2, dtype=f), np.ones((C, 1), f))
    c = np.eye(C, dtype=f) - f(1.0 / C)
    g = np.arange(G * K2) // K2
    return {
        "c_ident": np.eye(128, dtype=f),
        "c_centre": np.kron(np.eye(2, dtype=f), c),
        "c_mean": two / f(C),
        "c_head": np.kron(np.ones((2, 1), f), np.kron(np.eye(NH, dtype=f), np.ones((HD, 1), f))) * f(HD ** -0.5),
        "c_gsel": (g[:, None] == (np.arange(C) // (C // G))[None, :]).astype(f),
        "c_kmask": (np.arange(G * K2)[:, None] % K2 == np.arange(K2)[None, :]).astype(f),
    }


def kernel(**inputs):
    import numpy as _np
    import concourse.bacc as _bacc
    from concourse import mybir as _mybir
    from concourse.bass_utils import run_bass_kernel_spmd as _run

    nc = _bacc.Bacc("TRN2", target_bir_lowering=False, num_devices=1)
    arrays = {"x": _np.ascontiguousarray(inputs["x"])}
    for name in _INS:
        arrays[name] = _np.ascontiguousarray(inputs["L0_conv_" + name])
    for name in _INS1:
        arrays[name] = _np.ascontiguousarray(inputs["L1_conv_" + name])
    arrays["rpb_t"] = _np.ascontiguousarray(_np.asarray(inputs["L0_conv_rpb_table"]).T)
    arrays.update(constants())
    arrays = {"in_" + n: v for n, v in arrays.items()}
    aps = {n[3:]: nc.dram_tensor(n, v.shape, _mybir.dt.from_np(v.dtype), kind="ExternalInput").ap()
           for n, v in arrays.items()}
    out = nc.dram_tensor("out_0", arrays["in_x"].shape, _mybir.dt.float32, kind="ExternalOutput").ap()
    bass_window_block(nc, aps, out)
    r = _run(nc, [arrays], core_ids=[0])
    return r.results[0]["out_0"]
```

```python
from contextlib import ExitStack

import concourse.bass as bass
from concourse import mybir

F32 = mybir.dt.float32
BF16 = mybir.dt.bfloat16
F16 = mybir.dt.float16
ALU = mybir.AluOpType
ACT = mybir.ActivationFunctionType
AX = mybir.AxisListType

C = 64
WS = 8
NH = 4
HD = C // NH
HID = 256
IMG = 256
B = 8
PAIRS = B // 2
TILES = IMG // WS
TOK = WS * IMG
NW = IMG // WS
BANK = 512
NCH = TOK // BANK
ROUNDS = NW // 2
LN_EPS = 1e-5
BN_EPS = 1e-5
G = 8
K2 = 9
YROWS = 10 + IMG
Y0 = 9
HC = HID // 128
FLUSH_STEPS = 3 + 2 + 7 + 2 + 2 + 3 + 3
TAPS = [t for t in range(K2) if t != K2 // 2]
PE_TAPS = TAPS[:3]
ACT_TAP = TAPS[3]
DVE_TAPS = TAPS[4:]
HALF = WS // 2
CONV_STEPS = 8 + 1 + 8


def halves():
    return ((0, slice(0, 64)), (1, slice(64, 128)))


def bass_window_block(nc, a, out):
    with ExitStack() as ctx:
        def sb(name, shape, dt=F32):
            return ctx.enter_context(nc.sbuf_tensor(name, shape, dt))

        def sem(name):
            return ctx.enter_context(nc.semaphore(name))

        ident = sb("ident", [128, 128])
        ident_bf = sb("ident_bf", [128, 128], BF16)
        centre = sb("centre", [128, 128])
        mean_of = sb("mean_of", [128, 2])
        headmask = sb("headmask", [128, NH])
        gsel = sb("gsel", [G * K2, C])
        kmask = sb("kmask", [G * K2, K2])
        mean_all = sb("mean_all", [128, 128])
        pick_row = sb("pick_row", [96, 16, 128], BF16)
        pick_max = sb("pick_max", [128, NCH, 2, 8, 128], BF16)
        w_u = sb("w_u", [128, NH, 128])
        b_u = sb("b_u", [128, NH])
        w_v = sb("w_v", [128, C])
        w_p = sb("w_p", [128, 2, 2, 128])
        b_p = sb("b_p", [128, 1])
        w_1 = sb("w_1", [128, HID])
        b_1 = sb("b_1", [128, HC])
        w_2 = sb("w_2", [128, HC, C])
        b_y = sb("b_y", [128, 1])
        taps0 = sb("taps0", [128, K2])
        bias_t = sb("bias_t", [128, NH, 64])
        bias_s = sb("bias_s", [128, NH, 64], F16)
        twice = sb("twice", [128, 128], F16)
        bias_g = sb("bias_g", [128, 2, 64], BF16)
        cols = sb("cols", [128, 16])
        raw_w = sb("raw_w", [128, 3 * C])
        raw_p = sb("raw_p", [128, C])
        raw_1 = sb("raw_1", [128, HID])
        gain_w = sb("gain_w", [128, 3 * C])
        gain_1 = sb("gain_1", [128, HID])
        qk_t = sb("qk_t", [128, 2 * C])
        q_masked = sb("q_masked", [128, NH, C])
        vecs = sb("vecs", [128, 12])
        conv_w_t = sb("conv_w_t", [128, G * K2])
        bn = sb("bn", [G * K2, 8])
        lf = sb("lf", [G * K2, 2])
        lf_k = sb("lf_k", [G * K2, 2, K2])
        taps1 = sb("taps1", [128, K2])
        l1c = sb("l1c", [128, 8])
        const1 = sb("const1", [128, 1])
        half_neg = sb("half_neg", [128, 32])

        x_in = sb("x_in", [128, TOK])
        xb = sb("xb", [128, TOK])
        sq = sb("sq", [128, TOK])
        z1 = sb("z1", [128, NW, 64])
        z_bd = sb("z_bd", [128, NW, 128])
        u = sb("u", [128, NW, NH, 64])
        v = sb("v", [128, NW, 2, 2, 33])
        var = sb("var", [128, 32])
        rstd = sb("rstd", [128, 32])
        rstd3 = sb("rstd3", [128, 96], BF16)
        rstd_t = sb("rstd_t", [96, 128], BF16)
        zero32 = sb("zero32", [128, 32])
        mx = sb("mx", [128, 128], BF16)
        mx_t = sb("mx_t", [128, 128], BF16)
        rsum = sb("rsum", [128, 2, 8])
        o_n = sb("o_n", [128, 2, 128])
        o_t = sb("o_t", [128, 4, 128])
        x1 = sb("x1", [128, WS + 2, IMG + 2])
        z2 = sb("z2", [128, TOK])
        hid = sb("hid", [128, 2, 4, BANK])
        prob = hid[:, 0, :, :]
        f = sb("f", [128, WS + 1, IMG])
        acc = sb("acc", [128, 2])
        tot = sb("tot", [128, 1])
        mean2 = sb("mean2", [128, 2])
        flags = sb("flags", [128, 2])
        y_in = sb("y_in", [128, WS + 2, IMG + 2])
        res = sb("res", [128, WS, IMG])
        y_end = u[:, :, :, :].rearrange("p a b c -> p (a b c)")[:, 0:2 * 10 * 258].rearrange(
            "p (n r w) -> p n r w", n=2, r=10)
        res_end = hid[:, :, :, :].rearrange("p n j t -> p n (j t)").rearrange("p n (r w) -> p n r w", w=IMG)

        tap_end = (z2[:].rearrange("p (r w) -> p r w", w=IMG), xb[:].rearrange("p (r w) -> p r w", w=IMG))
        diag = sq[:, 0:len(PE_TAPS) * 128].rearrange("p (m c) -> p m c", c=128)

        ps = ctx.enter_context(nc.psum_tensor("ps", [128, 8, BANK], F32))
        stat_bank, proj_bank, s_bank, o_bank, t_bank = 2, 3, 4, 6, 7
        m_bank = stat_bank
        u_banks = (7, 3)
        f_banks = (2, 3, 6, 7)

        y_dram = nc.dram_tensor("y_scratch", [B, C, YROWS, IMG], F32, kind="Internal").ap()

        names = """const_loaded prep_mm prep_ev dve_chain dve_prep bn_root bn_var flush_chain pool_prep ready z_init
            x_loaded ln_mm ln_read squared stats var_ready rstd_ready pool_step rstd_tp rstd_copied
            zbd_ready u_mm u_ready guard_mm guard_max v_mm v_ready max_tp max_copied
            score_mm exp_done pv_mm o_recip o_ready o_tp o_copied proj_mm xb_ready x1_ready f1_mm gelu_done f2_mm
            f_ready conv_step f_shift f_centre y_done y_stored tot_step flush_step flush_done lf_mm lf_act lf_dve
            phase2_ready row_fix y_loaded edge_done tap_first tap_step res_done out_stored
            e_diag e_tap0 e_tap1 e_summed0 e_summed1 e_loaded0 e_loaded1 e_edge0 e_edge1 e_first0 e_first1 e_step0 e_step1 e_mm0 e_mm1
            e_read0 e_read1 e_done0 e_done1 e_stored0 e_stored1""".split()
        S = {n: sem(n) for n in names}

        xv = a["x"].rearrange("b c (i h) w -> b i c (h w)", h=WS)
        ctx.enter_context(nc.allow_non_contiguous_dma(reason="small weights"))
        block = ctx.enter_context(nc.Block())

        QB, PB, G1, B1N, G2, B2N, FB, DB, VB, KB = range(10)

        n_const = [0]

        @block.sync
        def _(sp):
            def ld(dst, src):
                sp.dma_start(dst, src).then_inc(S["const_loaded"], 16)
                n_const[0] += 16

            ld(ident[:], a["c_ident"])
            ld(centre[:], a["c_centre"])
            ld(mean_of[:], a["c_mean"])
            ld(headmask[:], a["c_head"])
            ld(gsel[:], a["c_gsel"])
            ld(kmask[:], a["c_kmask"])
            qkv_b = a["qkv_b"].rearrange("(k c o) -> k c o", k=3, o=1)

            def column(name):
                return a[name].rearrange("(c o) -> c o", o=1)

            for s, h in halves():
                ld(raw_w[h, :], a["qkv_w"])
                ld(raw_p[h, :], a["proj_w"])
                ld(raw_1[h, :], a["ffn_w1"])
                for k, src in ((QB, qkv_b[0]), (KB, qkv_b[1]), (VB, qkv_b[2]), (PB, column("proj_b")),
                               (G1, column("norm1_g")), (B1N, column("norm1_b")), (G2, column("norm2_g")),
                               (B2N, column("norm2_b")), (FB, column("ffn_w2_b")), (DB, column("dw_b"))):
                    ld(cols[h, k:k + 1], src)
                ld(taps0[h, :], a["dw_w"].rearrange("c o i j -> c (o i j)"))
                ld(l1c[h, 0:1], column("lamb_l"))
                ld(l1c[h, 1:2], column("lamb_h"))
                ld(l1c[h, 2:3], a["inside_all"].rearrange("c a b -> c (a b)"))
                ld(conv_w_t[h, :], a["conv_w"].rearrange("g c -> c g"))
            ld(b_1[:], a["ffn_b1"].rearrange("(k p) -> p k", k=HC))
            ld(w_2[:], a["ffn_w2"].rearrange("(k p) c -> p k c", k=HC))
            for k, name in enumerate(("bn_gamma", "bn_beta", "bn_mean", "bn_var")):
                ld(bn[:, k:k + 1], column(name))
            tab = a["rpb_t"]
            for m in range(64):
                r0, c0 = WS - 1 - m // WS, WS - 1 - m % WS
                src = tab.rearrange("h (r c) -> h r c", c=2 * WS - 1)[:, r0:r0 + WS, c0:c0 + WS]
                ld(bias_t[m:m + 1, :, :].rearrange("p h (r c) -> p h r c", c=WS),
                   src.rearrange("(o h) r c -> o h r c", o=1))
            sp.wait_ge(S["const_loaded"], n_const[0])
            ld(bias_t[64:128, :, :], bias_t[0:64, :, :])
            sp.wait_ge(S["z_init"], 1)
            for w in range(2):
                for h2 in range(2):
                    for s in range(2):
                        for hp in range(2):
                            p0 = 64 * w + 32 * hp + 16 * s
                            ld(w_p[p0:p0 + 16, w, h2, 64 * s:64 * s + 64],
                               a["proj_w"][HD * (2 * hp + h2):HD * (2 * hp + h2 + 1), :])

            def load_x(p, i):
                for s, h in halves():
                    sp.dma_start(x_in[h, :], xv[p + PAIRS * s, i, :, :]).then_inc(S["x_loaded"], 16)

            def fix_rows(p):
                sp.wait_ge(S["y_stored"], (p + 1) * 32 * (TILES + 2))
                for s in range(2):
                    yb = y_dram[p + PAIRS * s, :, :, :]
                    sp.dma_start(yb[:, Y0 - 1, :], yb[:, Y0 + 1, :]).then_inc(S["row_fix"], 16)
                    sp.dma_start(yb[:, Y0 + IMG, :], yb[:, Y0 + IMG - 2, :]).then_inc(S["row_fix"], 16)
                sp.wait_ge(S["row_fix"], (p + 1) * 64)

            def load_y(p, i, dst, signal):
                for s, h in halves():
                    sp.dma_start(dst[h, :, 1:257], y_dram[p + PAIRS * s, :, bass.ds(i * WS + Y0 - 1, WS + 2), :]
                                 ).then_inc(S[signal], 16)

            def store_res(p, i, src, signal):
                for s, h in halves():
                    sp.dma_start(out[p + PAIRS * s, :, bass.ds(i * WS, WS), :], src[h, :, :]).then_inc(S[signal], 16)

            def x_after(T, p, i):
                sp.wait_ge(S["xb_ready"], T + 2)
                sp.wait_ge(S["ln_read"], 16 * T + 12)
                load_x(p, i)

            def out_tile(N, p, i, more):
                sp.wait_ge(S["res_done"], N + 1)
                store_res(p, i, res, "out_stored")
                sp.wait_ge(S["out_stored"], 32 * N + 32)
                if more:
                    load_y(p, i + 1, y_in, "y_loaded")

            load_x(0, 0)
            sp.wait_ge(S["xb_ready"], 1)
            sp.wait_ge(S["ln_read"], 4)
            load_x(0, 1)
            with sp.Fori(0, TILES - 2) as i:
                x_after(i, 0, i + 2)
            x_after(TILES - 2, 1, 0)
            x_after(TILES - 1, 1, 1)
            fix_rows(0)
            load_y(0, 0, y_in, "y_loaded")
            with sp.Fori(1, PAIRS - 1) as p:
                with sp.Fori(0, TILES - 2) as i:
                    x_after(p * TILES + i, p, i + 2)
                    out_tile((p - 1) * TILES + i, p - 1, i, True)
                x_after(p * TILES + TILES - 2, p + 1, 0)
                out_tile((p - 1) * TILES + TILES - 2, p - 1, TILES - 2, True)
                x_after(p * TILES + TILES - 1, p + 1, 1)
                out_tile((p - 1) * TILES + TILES - 1, p - 1, TILES - 1, False)
                fix_rows(p)
                load_y(p, 0, y_in, "y_loaded")
            P3 = PAIRS - 1
            with sp.Fori(0, TILES - 2) as i:
                x_after(P3 * TILES + i, P3, i + 2)
                out_tile((P3 - 1) * TILES + i, P3 - 1, i, True)
            x_after(P3 * TILES + TILES - 2, 0, 0)
            out_tile((P3 - 1) * TILES + TILES - 2, P3 - 1, TILES - 2, True)
            out_tile((P3 - 1) * TILES + TILES - 1, P3 - 1, TILES - 1, False)
            fix_rows(P3)
            sp.wait_ge(S["phase2_ready"], PAIRS)
            for n in range(2):
                load_y(P3, n, y_end[:, n, :, :], f"e_loaded{n}")
            with sp.Fori(0, TILES // 2 - 1) as j:
                for n in range(2):
                    sp.wait_ge(S[f"e_done{n}"], j + 1)
                    sp.wait_ge(S[f"e_tap{n}"], j + 1)
                    load_y(P3, 2 * j + 2 + n, y_end[:, n, :, :], f"e_loaded{n}")
                    sp.wait_ge(S[f"e_summed{n}"], j + 1)
                    store_res(P3, 2 * j + n, res_end[:, n, :, :], f"e_stored{n}")
            for n in range(2):
                sp.wait_ge(S[f"e_summed{n}"], TILES // 2)
                store_res(P3, TILES - 2 + n, res_end[:, n, :, :], f"e_stored{n}")
            for n in range(2):
                sp.wait_ge(S[f"e_stored{n}"], 32 * (TILES // 2))
            sp.wait_ge(S["out_stored"], 32 * TILES * P3)

        @block.gpsimd
        def _(pool):
            add, sub = ALU.add, ALU.subtract
            nc.gpsimd.memset(half_neg[:], -0.5).then_inc(S["pool_prep"], 1)
            nc.gpsimd.memset(zero32[:], 0.0).then_inc(S["pool_prep"], 1)
            pool.wait_ge(S["pool_prep"], 2)
            pool.wait_ge(S["bn_var"], 1)
            nc.gpsimd.tensor_tensor(bn[:, 7:8], bn[:, 6:7], half_neg[0:G * K2, 0:1], ALU.pow).then_inc(S["bn_root"], 1)
            pool.wait_ge(S["ready"], 1)

            def root(n):
                tt = nc.gpsimd.tensor_tensor
                pool.wait_ge(S["var_ready"], n)
                tt(rstd[:], var[:], half_neg[:], ALU.pow).then_inc(S["pool_step"], 1)
                pool.wait_ge(S["pool_step"], 5 * n - 4)
                tt(rstd3[:, 0:32], rstd[:], zero32[:], add).then_inc(S["pool_step"], 1)
                pool.wait_ge(S["pool_step"], 5 * n - 3)
                tt(rstd[:], rstd[:], rstd3[:, 0:32], sub).then_inc(S["pool_step"], 1)
                pool.wait_ge(S["pool_step"], 5 * n - 2)
                tt(rstd3[:, 32:64], rstd[:], zero32[:], add).then_inc(S["pool_step"], 1)
                pool.wait_ge(S["pool_step"], 5 * n - 1)
                tt(rstd[:], rstd[:], rstd3[:, 32:64], sub).then_inc(S["pool_step"], 1)
                pool.wait_ge(S["pool_step"], 5 * n)
                tt(rstd3[:, 64:96], rstd[:], zero32[:], add).then_inc(S["rstd_ready"], 1)

            def residual_input(t):
                pool.wait_ge(S["x_loaded"], 32 * t + 32)
                nc.gpsimd.tensor_tensor(xb[:], x_in[:], b_p[:, 0:1].broadcast_to([128, TOK]),
                                        ALU.add).then_inc(S["xb_ready"], 1)

            residual_input(0)
            root(1)
            with pool.Fori(0, PAIRS) as p:
                with pool.Fori(0, TILES) as i:
                    T = p * TILES + i
                    root(2 * T + 2)
                    pool.wait_ge(S["x1_ready"], 4 * T + 4)
                    residual_input(T + 1)
                    root(2 * T + 3)
            with pool.Fori(0, TILES // 2) as j:
                for n in range(2):
                    pool.wait_ge(S[f"e_tap{n}"], j + 1)
                    pool.wait_ge(S[f"e_done{n}"], j + 1)
                    nc.gpsimd.tensor_tensor(res_end[:, n, :, :], res_end[:, n, :, :], tap_end[n],
                                            add).then_inc(S[f"e_summed{n}"], 1)

        @block.tensor
        def _(pe):
            mm = nc.tensor.matmul
            pe.wait_ge(S["dve_prep"], 1)
            M = ps[:, 7, :]
            for s, h in halves():
                mm(ps[h, 0, 0:64], gain_w[h, 0:64], centre[h, 64 * s:64 * s + 64], start=True, stop=True)
                mm(ps[h, 0, 64:128], gain_w[h, 64:128], centre[h, 64 * s:64 * s + 64], start=True, stop=True)
                mm(ps[h, 0, 128:192], centre[h, 64 * s:64 * s + 64], gain_w[h, 128:192], start=True, stop=True)
                mm(ps[h, 1, 0:HID], centre[h, 64 * s:64 * s + 64], gain_1[h, :], start=True, stop=True)
                for k in range(3):
                    mm(ps[h, 2, k:k + 1], raw_w[h, 64 * k:64 * k + 64], cols[h, B1N:B1N + 1], start=True, stop=True)
            for k in range(HC):
                mm(ps[:, 3, k:k + 1], raw_1[0:64, 128 * k:128 * k + 128], cols[0:64, B2N:B2N + 1],
                   start=True, stop=True)
            for hp in range(2):
                last = nc.tensor.transpose(ps[:, 4, 64 * hp:64 * hp + 64],
                                           bias_t[0:64, 2 * hp:2 * hp + 2, :].rearrange("p h n -> p (h n)"),
                                           ident[0:64, 0:64])
            last.then_inc(S["prep_mm"], 1)
            pe.wait_ge(S["prep_ev"], 1)
            for s, h in halves():
                for hh in range(NH):
                    mm(ps[h, 0, 64 * hh:64 * hh + 64], q_masked[h, hh, :], qk_t[h, 64:128], start=True, stop=True)
                    mm(ps[h, 1, hh:hh + 1], qk_t[h, 64:128], vecs[h, 4 + hh:5 + hh], start=True, stop=True)
                last = mm(ps[h, 2, 0:1], raw_p[h, :], vecs[h, 2:3], start=True, stop=True)
            last.then_inc(S["prep_mm"], 1)
            pe.wait_ge(S["ready"], 1)

            def hi(ap):
                return ap.bitcast(BF16)[:, 1::2]

            def norm_mean(base, n, rhs, first=False):
                if n >= 2 or not first:
                    pe.wait_ge(S["ln_read"], base + n - 1)
                mm(ps[:, n % 2, :], mean_all[:], rhs, start=True, stop=True).then_inc(S["ln_mm"], 1)

            def norm_stats(n, c):
                pe.wait_ge(S["squared"], 4 * n - 3 + c)
                for k in range(4 * c, 4 * c + 4):
                    last = mm(ps[:, stat_bank, 2 * k:2 * k + 2], sq[:, 128 * k:128 * k + 128], mean_of[:],
                              start=True, stop=True)
                if c == NCH - 1:
                    last.then_inc(S["stats"], 1)

            def norm_turn(n):
                pe.wait_ge(S["rstd_ready"], n)
                nc.tensor.transpose(ps[0:96, stat_bank, 64:128].bitcast(BF16), rstd3[:],
                                    ident_bf[:]).then_inc(S["rstd_tp"], 1)

            def norm_spread(base, n, ln, k, first=False):
                pe.wait_ge(S["rstd_copied"], ln)
                if n >= 2 or not first:
                    pe.wait_ge(S["ln_read"], base + n - 1)
                bank = n % 2
                for j in range(4):
                    last = mm(ps[:, bank, 128 * j:128 * j + 128], pick_row[:, 4 * k + j, :], rstd_t[:],
                              start=True, stop=True)
                last.then_inc(S["ln_mm"], 1)

            x_windows = x_in[:].rearrange("p (r w c) -> p w r c", r=WS, c=WS)
            z1_flat = z1[:].rearrange("p w t -> p (w t)")

            def x_chunk(k):
                return x_windows[:, 8 * k:8 * k + 8, :, :]

            def x1_chunk(k):
                return x1[:, 2 + 2 * k:4 + 2 * k, 1:257]

            def project_u(g, k, hh):
                n = 4 * k + hh
                if n >= 4:
                    pe.wait_ge(S["u_ready"], 16 * g + n - 1)
                mm(ps[:, u_banks[n % 2] if n >= 2 else s_bank + n, :], w_u[:, hh, :], z1_flat[:, BANK * k:BANK * k + BANK],
                   start=True, stop=True).then_inc(S["u_mm"], 1)
                if k:
                    guard(g, k - 1, hh)

            def project_v(g, k):
                pe.wait_ge(S["zbd_ready"], 4 * g + k + 1)
                if k:
                    pe.wait_ge(S["v_ready"], 4 * g + k)
                mm(ps[:, o_bank, 0:64], z_bd[:, 8 * k, :], w_v[:], start=True, stop=True)
                for w8 in range(1, 8):
                    for s, h in halves():
                        last = mm(ps[h, o_bank, 64 * w8:64 * w8 + 64], z1[h, 8 * k + w8, :], w_v[h, :],
                                  start=True, stop=True)
                last.then_inc(S["v_mm"], 1)

            def guard(g, k, j):
                n = 4 * k + j
                hp, w4 = j // 2, j % 2
                pe.wait_ge(S["u_ready"], 16 * g + 4 * k + 2 * hp + 2)
                if n >= 2:
                    pe.wait_ge(S["guard_max"], 16 * g + n - 1)
                bank = s_bank + n % 2
                mm(ps[:, bank, :], ident_bf[:], bias_g[:, hp:hp + 1, :].broadcast_to([128, 8, 64]),
                   start=True, stop=False, skip_group_check=True)
                for q in range(4):
                    w = 8 * k + 4 * w4 + q
                    last = mm(ps[:, bank, 128 * q:128 * q + 128],
                              hi(u[:, w, 2 * hp:2 * hp + 2, :].rearrange("p a n -> p (a n)")),
                              hi(z_bd[:, w, :]), start=False, stop=(q == 3), skip_group_check=True)
                last.then_inc(S["guard_mm"], 1)

            def max_turn(g):
                pe.wait_ge(S["guard_max"], 16 * g + 16)
                nc.tensor.transpose(ps[:, s_bank, 0:64].bitcast(BF16), mx[:], ident_bf[:]).then_inc(S["max_tp"], 1)

            def rounds(T):
                def scores(r):
                    bank = s_bank + r % 2
                    if r >= 2:
                        pe.wait_ge(S["exp_done"], 16 * T + r - 1)
                    mm(ps[:, bank, :], twice[:], bias_s[:].rearrange("p h n -> p (h n)").unsqueeze(1).broadcast_to(
                        [128, 2, 256]), start=True, stop=False, skip_group_check=True)
                    for w2 in range(2):
                        w = 2 * r + w2
                        for hp in range(2):
                            mm(ps[:, bank, 256 * w2 + 128 * hp:256 * w2 + 128 * hp + 128],
                               pick_max[:, w // 8, hp, w % 8, :], mx_t[:], start=False, stop=False,
                               skip_group_check=True)
                        last = mm(ps[:, bank, 256 * w2:256 * w2 + 256], z_bd[:, w, :],
                                  u[:, w, :, :].rearrange("p h n -> p (h n)"), start=False,
                                  stop=True, skip_group_check=True)
                    last.then_inc(S["score_mm"], 1)

                def values(r):
                    pe.wait_ge(S["exp_done"], 16 * T + r + 1)
                    if r:
                        pe.wait_ge(S["o_ready"], 32 * T + 2 * r)
                    for w2 in range(2):
                        for hp in range(2):
                            c = 66 * (2 * w2 + hp)
                            last = mm(ps[:, o_bank, c:c + 66],
                                      prob[:, r % 4, 256 * w2 + 128 * hp:256 * w2 + 128 * hp + 128],
                                      v[:, 2 * r + w2, hp, :, :].rearrange("p s d -> p (s d)"), start=True, stop=True)
                    last.then_inc(S["pv_mm"], 1)

                def turn(r):
                    pe.wait_ge(S["o_ready"], 32 * T + 2 * r + 2)
                    if r % 4 == 0 and r:
                        pe.wait_ge(S["o_copied"], 4 * T + r // 4)
                    nc.tensor.transpose(ps[:, t_bank, 128 * (r % 4):128 * (r % 4) + 128], o_n[:, r % 2, :],
                                        ident[:]).then_inc(S["o_tp"], 1)

                def project(q):
                    pe.wait_ge(S["o_copied"], 4 * T + q + 1)
                    if q:
                        pe.wait_ge(S["x1_ready"], 4 * T + q)
                    for w2 in range(2):
                        for h2 in range(2):
                            last = mm(ps[:, proj_bank, 256 * w2:256 * w2 + 256], w_p[:, w2, h2, :],
                                      o_t[:, :, 64 * h2:64 * h2 + 64], start=(h2 == 0), stop=(h2 == 1))
                    last.then_inc(S["proj_mm"], 1)

                PROJECT_AT = (7, 11, 15, ROUNDS + 2)
                for r in range(ROUNDS + 3):
                    if r < 2:
                        pe.wait_ge(S["f_ready"], 4 * T + r + 1)
                    if r < ROUNDS:
                        scores(r)
                    if r == 0:
                        pe.wait_ge(S["x_loaded"], 32 * T + 64)
                    if r in (0, 2, 4, 6):
                        norm_mean(8 + 16 * T, r // 2, x_chunk(r // 2))
                    if r in (3, 5, 7, 9):
                        norm_stats(2 * T + 2, (r - 3) // 2)
                    if r == ROUNDS - 2:
                        norm_turn(2 * T + 2)
                    if r == ROUNDS - 1:
                        norm_spread(8 + 16 * T, 4, 2 * T + 2, 0)
                    if r == ROUNDS:
                        norm_spread(8 + 16 * T, 5, 2 * T + 2, 1)
                    if r == ROUNDS + 1:
                        pe.wait_ge(S["ln_read"], 16 * T + 13)
                        project_u(T + 1, 0, 0)
                    if r == ROUNDS + 2:
                        project_u(T + 1, 0, 1)
                    if 1 <= r <= ROUNDS:
                        values(r - 1)
                    if 2 <= r <= ROUNDS + 1:
                        turn(r - 2)
                    if r in PROJECT_AT:
                        project(PROJECT_AT.index(r))

            def up(T, k):
                pe.wait_ge(S["ln_read"], 16 * T + 21 + k)
                for hc in range(HC):
                    for s, h in halves():
                        j = 2 * hc + s
                        if k:
                            pe.wait_ge(S["gelu_done"], 16 * T + 4 * (k - 1) + j + 1)
                        mm(ps[:, f_banks[j], :], w_1[h, 128 * hc:128 * hc + 128], z2[h, BANK * k:BANK * k + BANK],
                           start=True, stop=True).then_inc(S["f1_mm"], 1)

            def down(T, k):
                if k >= 2:
                    pe.wait_ge(S["f_ready"], 4 * T + k + 1)
                for s, h in halves():
                    for hc in range(HC):
                        j = 2 * hc + s
                        pe.wait_ge(S["gelu_done"], 16 * T + 4 * k + j + 1)
                        last = mm(ps[h, s_bank + k % 2, :], w_2[:, hc, :], hid[:, k % 2, j, :],
                                  start=(hc == 0), stop=(hc == HC - 1))
                last.then_inc(S["f2_mm"], 1)

            pe.wait_ge(S["x_loaded"], 32)
            for k in range(4):
                norm_mean(0, k, x_chunk(k), first=True)
            for k in range(4):
                norm_stats(1, k)
            norm_turn(1)
            for k in range(4):
                norm_spread(0, 4 + k, 1, k)
                pe.wait_ge(S["ln_read"], 5 + k)
                for hh in range(NH):
                    project_u(0, k, hh)
                project_v(0, k)
            for j in range(4):
                guard(0, 3, j)
            max_turn(0)

            with pe.Fori(0, PAIRS) as p:
                with pe.Fori(0, TILES) as i:
                    T = p * TILES + i
                    g = T + 1

                    X = 8 + 16 * T

                    pe.wait_ge(S["max_copied"], T + 1)
                    rounds(T)
                    project_u(g, 0, 2)
                    pe.wait_ge(S["x1_ready"], 4 * T + 4)
                    project_u(g, 0, 3)
                    project_v(g, 0)
                    norm_mean(X, 6, x1_chunk(0))
                    norm_mean(X, 7, x1_chunk(1))
                    pe.wait_ge(S["ln_read"], 16 * T + 14)
                    project_u(g, 1, 0)
                    project_u(g, 1, 1)
                    norm_spread(X, 8, 2 * T + 2, 2)
                    project_u(g, 1, 2)
                    project_u(g, 1, 3)
                    norm_mean(X, 9, x1_chunk(2))
                    project_v(g, 1)
                    norm_stats(2 * T + 3, 0)
                    norm_stats(2 * T + 3, 1)
                    norm_mean(X, 10, x1_chunk(3))
                    pe.wait_ge(S["ln_read"], 16 * T + 17)
                    project_u(g, 2, 0)
                    project_u(g, 2, 1)
                    norm_spread(X, 11, 2 * T + 2, 3)
                    project_u(g, 2, 2)
                    norm_stats(2 * T + 3, 2)
                    norm_stats(2 * T + 3, 3)
                    project_u(g, 2, 3)
                    project_v(g, 2)
                    pe.wait_ge(S["ln_read"], 16 * T + 20)
                    for hh in range(NH):
                        project_u(g, 3, hh)
                    project_v(g, 3)
                    guard(g, 3, 0)
                    guard(g, 3, 1)
                    norm_turn(2 * T + 3)
                    guard(g, 3, 2)
                    norm_spread(X, 12, 2 * T + 3, 0)
                    guard(g, 3, 3)
                    norm_spread(X, 13, 2 * T + 3, 1)
                    pe.wait_ge(S["v_ready"], 4 * g + 4)
                    up(T, 0)
                    max_turn(g)
                    norm_spread(X, 14, 2 * T + 3, 2)
                    up(T, 1)
                    norm_spread(X, 15, 2 * T + 3, 3)
                    pe.wait_ge(S["max_copied"], g + 1)
                    down(T, 0)
                    up(T, 2)
                    down(T, 1)
                    up(T, 3)
                    down(T, 2)
                    down(T, 3)
                pe.wait_ge(S["flush_done"], p + 1)
                mm(ps[0:G * K2, m_bank, 0:2], conv_w_t[:], mean2[:], start=True, stop=True).then_inc(S["lf_mm"], 1)
                pe.wait_ge(S["lf_dve"], 2 * p + 2)
                for s, h in halves():
                    last = mm(ps[h, m_bank, 64:64 + K2], gsel[:], lf_k[:, s, :], start=True, stop=True)
                last.then_inc(S["lf_mm"], 1)
                pe.wait_ge(S["phase2_ready"], p + 1)

            def second_taps(j, n, first):
                pe.wait_ge(S[f"e_edge{n}"], j + 1)
                if not first:
                    pe.wait_ge(S[f"e_done{n}"], j)
                for k in range(NCH):
                    for m, t in enumerate(PE_TAPS):
                        last = mm(ps[:, 4 * n + k, :], diag[:, m, :],
                                  y_end[:, n, t // 3 + 2 * k:t // 3 + 2 * k + 2, t % 3:t % 3 + IMG],
                                  start=(m == 0), stop=(m == len(PE_TAPS) - 1))
                    last.then_inc(S[f"e_mm{n}"], 1)

            pe.wait_ge(S["e_diag"], len(PE_TAPS))
            for n in range(2):
                second_taps(0, n, True)
            with pe.Fori(1, TILES // 2) as j:
                for n in range(2):
                    second_taps(j, n, False)

        @block.scalar
        def _(act):
            actf = nc.scalar.activation

            def store_y(p, i, rows, r0=0):
                for s, h in halves():
                    act.dma_start(y_dram[p + PAIRS * s, :, bass.ds(i * WS, rows), :],
                                  f[h, r0:r0 + rows, :]).then_inc(S["y_stored"], 16)

            act.wait_ge(S["ready"], 1)

            def square(k, d, read):
                act.wait_ge(S["ln_read"], read)
                actf(sq[:, BANK * k:BANK * k + BANK], d[:, BANK * k:BANK * k + BANK], ACT.Square).then_inc(
                    S["squared"], 1)

            def copy_rstd(n):
                act.wait_ge(S["rstd_tp"], n)
                actf(rstd_t[:], ps[0:96, stat_bank, 64:128].bitcast(BF16), ACT.Copy).then_inc(S["rstd_copied"], 1)

            z1_flat = z1[:].rearrange("p w t -> p (w t)")

            def diagonal(k, read):
                act.wait_ge(S["ln_read"], read)
                for s, h in halves():
                    last = actf(z_bd[h, 8 * k:8 * k + 8, 64 * s:64 * s + 64], z1[h, 8 * k:8 * k + 8, :], ACT.Copy)
                last.then_inc(S["zbd_ready"], 1)

            def take_uv(g, k, read, beside=None, early=None):
                for hh in range(NH):
                    n = 4 * k + hh
                    act.wait_ge(S["u_mm"], 16 * g + n + 1)
                    bank = u_banks[n % 2] if n >= 2 else s_bank + n
                    actf(u[:, 8 * k:8 * k + 8, hh, :], ps[:, bank, :].rearrange("p (w n) -> p w n", w=8),
                         ACT.Identity, bias=b_u[:, hh:hh + 1]).then_inc(S["u_ready"], 1)
                    if hh == 0:
                        if early:
                            early()
                        diagonal(k, read)
                    if beside:
                        beside(k, hh)
                act.wait_ge(S["v_mm"], 4 * g + k + 1)
                for s, h in halves():
                    last = actf(v[h, 8 * k:8 * k + 8, :, s, 0:32],
                                ps[h, o_bank, :].rearrange("p (w a d) -> p w a d", w=8, a=2), ACT.Copy)
                last.then_inc(S["v_ready"], 1)

            def copy_max(g):
                act.wait_ge(S["max_tp"], g + 1)
                actf(mx_t[:], ps[:, s_bank, 0:64].bitcast(BF16), ACT.Copy).then_inc(S["max_copied"], 1)

            for k in range(4):
                square(k, z1_flat, k + 1)
            copy_rstd(1)
            for k in range(4):
                take_uv(0, k, 5 + k)
            copy_max(0)

            def body(T, p, i, second):
                g = T + 1

                def copy_o(q):
                    act.wait_ge(S["o_tp"], 16 * T + 4 * q + 4)
                    if q:
                        act.wait_ge(S["proj_mm"], 4 * T + q)
                    actf(o_t[:, :, :].rearrange("p a b -> p (a b)"), ps[:, t_bank, :],
                         ACT.Copy).then_inc(S["o_copied"], 1)

                for r in range(ROUNDS):
                    if r == ROUNDS - 1:
                        copy_rstd(2 * T + 2)
                    act.wait_ge(S["score_mm"], 16 * T + r + 1)
                    if r >= 4:
                        act.wait_ge(S["pv_mm"], 16 * T + r - 3)
                    actf(prob[:, r % 4, :], ps[:, s_bank + r % 2, :], ACT.Exp).then_inc(S["exp_done"], 1)
                    if r >= 6 and (r - 6) % 4 == 0:
                        copy_o((r - 6) // 4)
                    if r in (2, 4, 6, 8):
                        square(r // 2 - 1, z1_flat, 16 * T + 8 + r // 2)
                    if r == 9:
                        act.wait_ge(S["conv_step"], CONV_STEPS * T + 8)
                        actf(f[:, 0, :], f[:, 0, :], ACT.Identity, bias=b_y[:, 0:1], accum_out=acc[:, 0:1])
                    if r == 10:
                        actf(f[:, 1:WS, :], f[:, 1:WS, :], ACT.Identity, bias=b_y[:, 0:1],
                             accum_out=acc[:, 1:2]).then_inc(S["y_done"], 1)
                    if second and r == 11:
                        act.wait_ge(S["y_loaded"], 32 * (T - TILES) + 32)
                        actf(res[:], y_in[:, 1:9, 1:257], ACT.Identity, bias=const1[:, 0:1],
                             scale=taps1[:, 4:5]).then_inc(S["tap_first"], 1)
                    if r == 14:
                        act.wait_ge(S["y_done"], T + 1)
                        store_y(p, i, WS)
                def beside(k, hh):
                    if (k, hh) == (0, 1):
                        act.wait_ge(S["y_stored"], 32 * (T + 2 * p + 1))
                        actf(f[:, 0, :], f[:, WS, :], ACT.Copy).then_inc(S["f_shift"], 1)
                    if (k, hh) == (0, 3):
                        act.wait_ge(S["x1_ready"], 4 * T + 4)
                        actf(f[:, 1:5, :], x1[:, 2:6, 1:257], ACT.Copy, scale=taps0[:, 4:5]).then_inc(
                            S["f_centre"], 1)
                    if (k, hh) == (1, 3):
                        act.wait_ge(S["f_shift"], T + 1)
                        actf(f[:, 5:9, :], x1[:, 6:10, 1:257], ACT.Copy, scale=taps0[:, 4:5]).then_inc(
                            S["f_centre"], 1)
                    if (k, hh) in ((1, 1), (1, 2), (2, 0), (2, 1)):
                        c = 2 * (k - 1) + hh - (k == 1)
                        square(c, z2, 16 * T + (15, 16, 18, 19)[c])

                for k in range(NCH):
                    take_uv(g, k, 16 * T + (13, 14, 17, 20)[k], beside, (lambda: copy_o(3)) if k == 0 else None)
                copy_rstd(2 * T + 3)
                for k in range(NCH):
                    for j in range(4):
                        act.wait_ge(S["f1_mm"], 16 * T + 4 * k + j + 1)
                        if k >= 2 and j == 0:
                            act.wait_ge(S["f2_mm"], 4 * T + k - 1)
                        actf(hid[:, k % 2, j, :], ps[:, f_banks[j], :], ACT.Gelu,
                             bias=b_1[:, j // 2:j // 2 + 1]).then_inc(S["gelu_done"], 1)
                    if k == 0:
                        copy_max(g)

            def flush(p):
                act.wait_ge(S["flush_step"], 2 * p + 1)
                actf(f[:, 0, :], f[:, 0, :], ACT.Identity, bias=b_y[:, 0:1], accum_out=acc[:, 0:1])
                actf(f[:, 1:WS, :], f[:, 1:WS, :], ACT.Identity, bias=b_y[:, 0:1],
                     accum_out=acc[:, 1:2]).then_inc(S["lf_act"], 1)
                act.wait_ge(S["lf_act"], 3 * p + 1)
                store_y(p, TILES, WS)
                act.wait_ge(S["flush_step"], 2 * p + 2)
                actf(f[:, WS, :], f[:, WS, :], ACT.Identity, bias=b_y[:, 0:1],
                     accum_out=acc[:, 0:1]).then_inc(S["lf_act"], 1)
                act.wait_ge(S["lf_act"], 3 * p + 2)
                store_y(p, TILES + 1, 1, WS)
                act.wait_ge(S["lf_dve"], 2 * p + 1)
                actf(lf[:], lf[:], ACT.Tanh).then_inc(S["lf_act"], 1)

            with act.Fori(0, TILES) as i:
                body(i, 0, i, False)
            flush(0)
            with act.Fori(1, PAIRS) as p:
                with act.Fori(0, TILES) as i:
                    body(p * TILES + i, p, i, True)
                flush(p)
            act.wait_ge(S["phase2_ready"], PAIRS)

            def second_first(j, n, first):
                y = y_end[:, n, :, :]
                act.wait_ge(S[f"e_loaded{n}"], 32 * j + 32)
                actf(y[:, :, 0:1], y[:, :, 2:3], ACT.Copy)
                actf(y[:, :, 257:258], y[:, :, 255:256], ACT.Copy).then_inc(S[f"e_edge{n}"], 1)
                if not first:
                    act.wait_ge(S[f"e_stored{n}"], 32 * j)
                actf(res_end[:, n, :, :], y[:, 1:9, 1:257], ACT.Identity, bias=const1[:, 0:1],
                     scale=taps1[:, 4:5]).then_inc(S[f"e_first{n}"], 1)
                t = ACT_TAP
                act.wait_ge(S[f"e_edge{n}"], j + 1)
                actf(tap_end[n], y[:, t // 3:t // 3 + WS, t % 3:t % 3 + IMG], ACT.Copy,
                     scale=taps1[:, t:t + 1]).then_inc(S[f"e_tap{n}"], 1)

            for n in range(2):
                second_first(0, n, True)
            with act.Fori(1, TILES // 2) as j:
                for n in range(2):
                    second_first(j, n, False)

        @block.vector
        def _(dve):
            V = nc.vector
            step = [0]

            def chain(ins):
                step[0] += 1
                ins.then_inc(S["dve_chain"], 1)
                dve.wait_ge(S["dve_chain"], step[0])

            chain(V.memset(w_p[:].rearrange("p a b c -> p (a b c)"), 0.0))
            V.memset(w_u[:].rearrange("p a b -> p (a b)"), 0.0).then_inc(S["z_init"], 1)
            chain(V.memset(x1[:].rearrange("p a b -> p (a b)"), 0.0))
            chain(V.memset(v[:].rearrange("p w a s d -> p (w a s d)"), 0.0))
            for s, h in halves():
                chain(V.memset(v[h, :, :, s, 32:33], 1.0))
            chain(V.memset(z_bd[:].rearrange("p w t -> p (w t)"), 0.0))
            chain(V.memset(f[:].rearrange("p a b -> p (a b)"), 0.0))
            dve.wait_ge(S["const_loaded"], n_const[0])
            chain(V.tensor_copy(ident_bf[:], ident[:]))
            for j in range(3):
                chain(V.tensor_copy(pick_row[32 * j:32 * j + 32, :, :].rearrange("r k (s c) -> r (k s) c", s=2),
                                    ident[32 * j:32 * j + 32, 32 * j:32 * j + 32].unsqueeze(2).broadcast_to([32, 32, 64])))
            chain(V.tensor_scalar(mean_all[:].rearrange("p (s c) -> p s c", s=2),
                                  mean_of[:].unsqueeze(2).broadcast_to([128, 2, 64]), 1.0, None, ALU.mult))
            for s, h in halves():
                chain(V.tensor_scalar(twice[h, :].rearrange("p (a m) -> p a m", a=2),
                                      ident[h, 64 * s:64 * s + 64].unsqueeze(1).broadcast_to([64, 2, 64]),
                                      1.0 if s == 0 else 2.0 ** -11, None, ALU.mult))
            for k in range(NCH):
                for hp in range(2):
                    for s in range(2):
                        i0 = 32 * k + 16 * hp + s
                        V.tensor_scalar(pick_max[:, k, hp, :, 64 * s:64 * s + 64],
                                        ident[:, i0:i0 + 15:2].unsqueeze(2).broadcast_to([128, 8, 64]),
                                        -1.0, None, ALU.mult)
            rest = sq[:, 0:256].rearrange("p (h n) -> p h n", h=NH)
            chain(V.tensor_copy(bias_s[:], bias_t[:]))
            chain(V.tensor_tensor(rest, bias_t[:], bias_s[:], ALU.subtract))
            chain(V.tensor_scalar(bias_s[64:128, :, :], rest[64:128, :, :], 2.0 ** 11, None, ALU.mult))
            chain(V.tensor_scalar(gain_w[:], raw_w[:], cols[:, G1:G1 + 1], None, ALU.mult))
            V.tensor_scalar(gain_1[:], raw_1[:], cols[:, G2:G2 + 1], None, ALU.mult).then_inc(S["dve_prep"], 1)
            dve.wait_ge(S["prep_mm"], 1)
            chain(V.tensor_copy(qk_t[:], ps[:, 0, 0:128]))
            chain(V.tensor_copy(w_v[:], ps[:, 0, 128:192]))
            chain(V.tensor_copy(w_1[:], ps[:, 1, 0:HID]))
            chain(V.tensor_tensor(vecs[:, 0:1], ps[:, 2, 0:1], cols[:, QB:QB + 1], ALU.add))
            chain(V.tensor_tensor(vecs[:, 2:3], ps[:, 2, 2:3], cols[:, VB:VB + 1], ALU.add))
            chain(V.tensor_tensor(b_1[:], b_1[:], ps[:, 3, 0:HC], ALU.add))
            chain(V.tensor_copy(bias_g[:], ps[:, 4, 0:128].rearrange("p (a m) -> p a m", a=2)))
            for hh in range(NH):
                chain(V.tensor_scalar(q_masked[:, hh, :], qk_t[:, 0:64], headmask[:, hh:hh + 1], None, ALU.mult))
            chain(V.tensor_scalar(vecs[:, 4:8], headmask[:], vecs[:, 0:1], None, ALU.mult))
            V.memset(vecs[:, 8:9], 0.0).then_inc(S["prep_ev"], 1)
            dve.wait_ge(S["prep_mm"], 2)
            for s, h in halves():
                chain(V.tensor_copy(w_u[h, :, 64 * s:64 * s + 64],
                                    ps[h, 0, 0:256].rearrange("p (h c) -> p h c", h=NH)))
            chain(V.tensor_copy(b_u[:], ps[:, 1, 0:NH]))
            chain(V.tensor_tensor(b_p[:], ps[:, 2, 0:1], cols[:, PB:PB + 1], ALU.add))
            chain(V.tensor_tensor(b_y[:], cols[:, FB:FB + 1], cols[:, DB:DB + 1], ALU.add))
            chain(V.tensor_scalar(taps0[:, 4:5], taps0[:, 4:5], 1.0, None, ALU.add))
            chain(V.scalar_tensor_tensor(l1c[:, 3:4], l1c[:, 2:3], 1.0, l1c[:, 0:1], ALU.add, ALU.mult))
            chain(V.tensor_scalar(l1c[:, 4:5], l1c[:, 1:2], 1.0, None, ALU.add))
            chain(V.scalar_tensor_tensor(l1c[:, 5:6], l1c[:, 2:3], -1.0, l1c[:, 0:1], ALU.mult, ALU.mult))
            V.tensor_scalar(bn[:, 6:7], bn[:, 3:4], BN_EPS, None, ALU.add).then_inc(S["bn_var"], 1)
            V.memset(tot[:], 0.0).then_inc(S["f_ready"], 2)
            chain(V.memset(flags[:], 0.0))
            dve.wait_ge(S["bn_root"], 1)
            chain(V.tensor_tensor(bn[:, 4:5], bn[:, 0:1], bn[:, 7:8], ALU.mult))
            chain(V.tensor_tensor(bn[:, 6:7], bn[:, 2:3], bn[:, 4:5], ALU.mult))
            chain(V.tensor_tensor(bn[:, 5:6], bn[:, 1:2], bn[:, 6:7], ALU.subtract))
            V.memset(acc[:], 0.0).then_inc(S["ready"], 1)

            def d1(n, k):
                dve.wait_ge(S["ln_mm"], n)
                xp = x_in[:].rearrange("p (r w c) -> p w r c", r=WS, c=WS)[:, 8 * k:8 * k + 8, :, :]
                V.tensor_tensor(z1[:, 8 * k:8 * k + 8, :].rearrange("p w (r c) -> p w r c", c=WS), xp,
                                ps[:, k % 2, :].rearrange("p (w r c) -> p w r c", w=8, c=WS),
                                ALU.subtract).then_inc(S["ln_read"], 1)

            def variance(n):
                dve.wait_ge(S["stats"], n)
                V.tensor_scalar(var[:], ps[:, stat_bank, 0:32], LN_EPS, None, ALU.add).then_inc(S["var_ready"], 1)

            def apply1(n, bank, k):
                dve.wait_ge(S["ln_mm"], n)
                zk = z1[:, 8 * k:8 * k + 8, :].rearrange("p w t -> p (w t)")
                V.tensor_tensor(zk, zk, ps[:, bank, :], ALU.mult).then_inc(S["ln_read"], 1)

            def row_max(g, k, j):
                n = 4 * k + j
                dve.wait_ge(S["guard_mm"], 16 * g + n + 1)
                V.tensor_reduce(mx[:, 8 * n:8 * n + 8], ps[:, s_bank + n % 2, :].rearrange("p (w m) -> p w m", w=8),
                                AX.X, ALU.max).then_inc(S["guard_max"], 1)

            def residual(T, q):
                dve.wait_ge(S["proj_mm"], 4 * T + q + 1)
                dve.wait_ge(S["xb_ready"], T + 1)
                for w2 in range(2):
                    w0 = 8 * q + w2
                    last = V.tensor_tensor(
                        x1[:, 2:10, 1:257].rearrange("p r (w c) -> p w r c", c=WS)[:, w0:w0 + 7:2, :, :],
                        ps[:, proj_bank, 256 * w2:256 * w2 + 256].rearrange("p (w r c) -> p w r c", w=4, r=WS),
                        xb[:].rearrange("p (r w c) -> p w r c", r=WS, c=WS)[:, w0:w0 + 7:2, :, :],
                        ALU.add)
                last.then_inc(S["x1_ready"], 1)

            def conv_tap(n, rows, src, dst, wait):
                t = TAPS[n]
                return V.scalar_tensor_tensor(dst, src[:, t // 3:t // 3 + rows, t % 3:t % 3 + IMG],
                                              wait[:, t:t + 1], dst, ALU.mult, ALU.add)

            dve.wait_ge(S["x_loaded"], 32)
            for k in range(4):
                d1(k + 1, k)
            variance(1)
            for k in range(4):
                apply1(5 + k, k % 2, k)
                if k:
                    for j in range(4):
                        row_max(0, k - 1, j)
            for j in range(4):
                row_max(0, 3, j)

            def body(T, second):
                g = T + 1
                X = 8 + 16 * T
                N = T - TILES

                def d2(n, k):
                    dve.wait_ge(S["ln_mm"], X + n + 1)
                    V.tensor_tensor(z2[:, BANK * k:BANK * k + BANK].rearrange("p (r w) -> p r w", r=2),
                                    x1[:, 2 + 2 * k:4 + 2 * k, 1:257],
                                    ps[:, n % 2, :].rearrange("p (r w) -> p r w", r=2),
                                    ALU.subtract).then_inc(S["ln_read"], 1)

                def apply2(n, k):
                    dve.wait_ge(S["ln_mm"], X + n + 1)
                    zk = z2[:, BANK * k:BANK * k + BANK]
                    V.tensor_tensor(zk, zk, ps[:, n % 2, :], ALU.mult).then_inc(S["ln_read"], 1)

                def conv_half(m, before, known=False):
                    if not known:
                        dve.wait_ge(S["conv_step"], before - 1)
                    r0 = HALF * (m % 2)
                    conv_tap(m // 2, HALF, x1[:, r0:r0 + HALF + 2, :], f[:, r0:r0 + HALF, :], taps0).then_inc(
                        S["conv_step"], 1)

                def second_half(m):
                    if m == 0:
                        dve.wait_ge(S["tap_first"], N + 1)
                        dve.wait_ge(S["edge_done"], N + 1)
                    elif m > 1:
                        dve.wait_ge(S["tap_step"], 15 * N + m - (m < 15))
                    r0 = HALF * (m % 2)
                    conv_tap(m // 2, HALF, y_in[:, r0:r0 + HALF + 2, :], res[:, r0:r0 + HALF, :], taps1).then_inc(
                        S["tap_step" if m < 15 else "res_done"], 1)

                for r in range(ROUNDS):
                    if r in (1, 3, 5, 7):
                        if r == 1:
                            dve.wait_ge(S["x_loaded"], 32 * T + 64)
                        d1(X + r // 2 + 1, r // 2)
                    dve.wait_ge(S["pv_mm"], 16 * T + r + 1)
                    O = ps[:, o_bank, 0:264].rearrange("p (g d) -> p g d", d=33)
                    V.reciprocal(rsum[:, r % 2, :], O[:, :, 32:33].rearrange("p g o -> p (g o)")).then_inc(
                        S["o_recip"], 1)
                    dve.wait_ge(S["o_recip"], 16 * T + r + 1)
                    if r >= 2:
                        dve.wait_ge(S["o_tp"], 16 * T + r - 1)
                    for h2, h in halves():
                        V.tensor_tensor(o_n[h, r % 2, :].rearrange("p (g d) -> p g d", d=HD),
                                        O[h, :, 16 * h2:16 * h2 + 16],
                                        rsum[h, r % 2, :].unsqueeze(2).broadcast_to([64, 8, HD]),
                                        ALU.mult).then_inc(S["o_ready"], 1)
                    if r < 8:
                        conv_half(8 + r, CONV_STEPS * T + r, known=r < 2)
                    if r == 8:
                        dve.wait_ge(S["conv_step"], CONV_STEPS * T + 8)
                        V.tensor_copy(x1[:, 0:2, :], x1[:, 8:10, :]).then_inc(S["conv_step"], 1)
                        dve.wait_ge(S["conv_step"], CONV_STEPS * T + 9)
                    if r == 9:
                        variance(2 * T + 2)
                    if r in (9, 12, 15):
                        residual(T, (r - 9) // 3)
                    if second and r == 11:
                        dve.wait_ge(S["y_loaded"], 32 * N + 32)
                        V.tensor_copy(y_in[:, :, 0:1], y_in[:, :, 2:3])
                        V.tensor_copy(y_in[:, :, 257:258], y_in[:, :, 255:256]).then_inc(S["edge_done"], 1)
                    if second and r >= 12:
                        second_half(r - 12)
                    if r == 14:
                        apply1(X + 5, 0, 0)
                apply1(X + 6, 1, 1)
                residual(T, 3)
                dve.wait_ge(S["x1_ready"], 4 * T + 4)
                d2(6, 0)
                d2(7, 1)
                row_max(g, 0, 0)
                row_max(g, 0, 1)
                apply1(X + 9, 0, 2)
                row_max(g, 0, 2)
                row_max(g, 0, 3)
                d2(9, 2)
                d2(10, 3)
                row_max(g, 1, 0)
                row_max(g, 1, 1)
                apply1(X + 12, 1, 3)
                done = CONV_STEPS * T + 9
                dve.wait_ge(S["f_shift"], T + 1)
                dve.wait_ge(S["f_centre"], 2 * T + 2)
                conv_half(0, done)
                conv_half(1, done + 1)
                row_max(g, 1, 2)
                conv_half(2, done + 2)
                row_max(g, 1, 3)
                conv_half(3, done + 3)
                variance(2 * T + 3)
                for j in range(4):
                    row_max(g, 2, j)
                    if j in (0, 2):
                        conv_half(4 + j // 2, done + 4 + j // 2)
                row_max(g, 3, 0)
                row_max(g, 3, 1)
                row_max(g, 3, 2)
                apply2(12, 0)
                row_max(g, 3, 3)
                apply2(13, 1)
                dve.wait_ge(S["y_done"], T + 1)
                V.scalar_tensor_tensor(tot[:], acc[:, 0:1], flags[:, 0:1], tot[:], ALU.mult, ALU.add).then_inc(
                    S["tot_step"], 1)
                dve.wait_ge(S["tot_step"], 4 * T + 1)
                V.scalar_tensor_tensor(tot[:], acc[:, 1:2], flags[:, 1:2], tot[:], ALU.mult, ALU.add).then_inc(
                    S["tot_step"], 1)
                V.tensor_copy(flags[:, 0:1], flags[:, 1:2]).then_inc(S["tot_step"], 1)
                dve.wait_ge(S["tot_step"], 4 * T + 3)
                V.memset(flags[:, 1:2], 1.0).then_inc(S["tot_step"], 1)
                beside = [2, 3, 4, 3, 0] if second else [0] * 5
                m2 = 4

                def second_halves():
                    nonlocal m2
                    for _ in range(beside.pop(0)):
                        second_half(m2)
                        m2 += 1

                conv_half(6, done + 6)
                conv_half(7, done + 7)
                apply2(14, 2)
                second_halves()
                apply2(15, 3)
                second_halves()
                dve.wait_ge(S["conv_step"], CONV_STEPS * T + CONV_STEPS)
                dve.wait_ge(S["tot_step"], 4 * T + 4)
                for k in range(NCH):
                    dve.wait_ge(S["f2_mm"], 4 * T + k + 1)
                    fk = f[:, 1 + 2 * k:3 + 2 * k, :]
                    V.tensor_tensor(fk, fk, ps[:, s_bank + k % 2, :].rearrange("p (r w) -> p r w", r=2),
                                    ALU.add).then_inc(S["f_ready"], 1)
                    if k < 3:
                        second_halves()
                dve.wait_ge(S["f_ready"], 4 * T + 6)

            def finish(p):
                n_fl = [0]

                def flush(ins):
                    n_fl[0] += 1
                    ins.then_inc(S["flush_chain"], 1)
                    dve.wait_ge(S["flush_chain"], FLUSH_STEPS * p + n_fl[0])

                dve.wait_ge(S["f_ready"], 4 * TILES * (p + 1) + 2)
                for n in range(4, 7):
                    flush(conv_tap(n, WS, x1, f[:, 0:WS, :], taps0))
                conv_tap(7, WS, x1, f[:, 0:WS, :], taps0).then_inc(S["flush_step"], 1)
                flush(V.tensor_copy(x1[:, 0:2, :], x1[:, 8:10, :]))
                flush(V.memset(x1[:, 2, :], 0.0))
                for n in range(7):
                    flush(conv_tap(n, 1, x1, f[:, WS:WS + 1, :], taps0))
                dve.wait_ge(S["lf_act"], 3 * p + 1)
                flush(V.tensor_tensor(tot[:], tot[:], acc[:, 0:1], ALU.add))
                flush(V.tensor_tensor(tot[:], tot[:], acc[:, 1:2], ALU.add))
                conv_tap(7, 1, x1, f[:, WS:WS + 1, :], taps0).then_inc(S["flush_step"], 1)
                dve.wait_ge(S["lf_act"], 3 * p + 2)
                flush(V.tensor_tensor(tot[:], tot[:], acc[:, 0:1], ALU.add))
                flush(V.tensor_scalar(tot[:], tot[:], 1.0 / (IMG * IMG), None, ALU.mult))
                V.tensor_scalar(mean2[:], mean_of[:], tot[:, 0:1], float(C), ALU.mult, ALU.mult).then_inc(
                    S["flush_done"], 1)
                dve.wait_ge(S["lf_mm"], 2 * p + 1)
                V.tensor_scalar(lf[:], ps[0:G * K2, m_bank, 0:2], bn[:, 4:5], bn[:, 5:6], ALU.mult,
                                ALU.add).then_inc(S["lf_dve"], 1)
                dve.wait_ge(S["lf_act"], 3 * p + 3)
                V.tensor_scalar(lf_k[:, 0, :], kmask[:], lf[:, 0:1], None, ALU.mult)
                V.tensor_scalar(lf_k[:, 1, :], kmask[:], lf[:, 1:2], None, ALU.mult).then_inc(S["lf_dve"], 1)
                dve.wait_ge(S["lf_mm"], 2 * p + 2)
                flush(V.tensor_scalar(taps1[:], ps[:, m_bank, 64:64 + K2], l1c[:, 3:4], None, ALU.mult))
                flush(V.tensor_tensor(taps1[:, 4:5], taps1[:, 4:5], l1c[:, 4:5], ALU.add))
                flush(V.tensor_tensor(const1[:], tot[:], l1c[:, 5:6], ALU.mult))
                flush(V.memset(tot[:], 0.0))
                flush(V.memset(flags[:], 0.0))
                dve.wait_ge(S["y_stored"], 32 * (TILES + 2) * (p + 1))
                flush(V.memset(f[:].rearrange("p a b -> p (a b)"), 0.0))
                V.memset(x1[:].rearrange("p a b -> p (a b)"), 0.0).then_inc(S["phase2_ready"], 1)
                assert n_fl[0] == FLUSH_STEPS

            with dve.Fori(0, TILES) as i:
                body(i, False)
            finish(0)
            with dve.Fori(1, PAIRS) as p:
                with dve.Fori(0, TILES) as i:
                    body(p * TILES + i, True)
                finish(p)
            for m, t in enumerate(PE_TAPS):
                V.tensor_scalar(diag[:, m, :], ident[:], taps1[:, t:t + 1], None, ALU.mult).then_inc(S["e_diag"], 1)
            with dve.Fori(0, TILES // 2) as j:
                for n in range(2):
                    y, r, nt = y_end[:, n, :, :], res_end[:, n, :, :], len(DVE_TAPS)
                    dve.wait_ge(S[f"e_edge{n}"], j + 1)
                    dve.wait_ge(S[f"e_first{n}"], j + 1)
                    for m, t in enumerate(DVE_TAPS):
                        V.scalar_tensor_tensor(r, y[:, t // 3:t // 3 + WS, t % 3:t % 3 + IMG], taps1[:, t:t + 1], r,
                                               ALU.mult, ALU.add).then_inc(S[f"e_step{n}"], 1)
                        dve.wait_ge(S[f"e_step{n}"], nt * j + m + 1)
                    for k in range(NCH):
                        dve.wait_ge(S[f"e_mm{n}"], NCH * j + k + 1)
                        rk = r[:, 2 * k:2 * k + 2, :]
                        if k == NCH - 1:
                            dve.wait_ge(S[f"e_read{n}"], (NCH - 1) * (j + 1))
                        V.tensor_tensor(rk, rk, ps[:, 4 * n + k, :].rearrange("p (r w) -> p r w", r=2),
                                        ALU.add).then_inc(S[f"e_read{n}" if k < NCH - 1 else f"e_done{n}"], 1)


_INS = ["qkv_w", "proj_w", "ffn_w1", "ffn_w2", "qkv_b", "proj_b", "norm1_g", "norm1_b", "norm2_g", "norm2_b",
        "ffn_b1", "ffn_w2_b", "dw_w", "dw_b"]
_INS1 = ["conv_w", "bn_gamma", "bn_beta", "bn_mean", "bn_var", "lamb_l", "lamb_h", "inside_all"]


def constants():
    import numpy as np
    f = np.float32
    two = np.kron(np.eye(2, dtype=f), np.ones((C, 1), f))
    c = np.eye(C, dtype=f) - f(1.0 / C)
    g = np.arange(G * K2) // K2
    return {
        "c_ident": np.eye(128, dtype=f),
        "c_centre": np.kron(np.eye(2, dtype=f), c),
        "c_mean": two / f(C),
        "c_head": np.kron(np.ones((2, 1), f), np.kron(np.eye(NH, dtype=f), np.ones((HD, 1), f))) * f(HD ** -0.5),
        "c_gsel": (g[:, None] == (np.arange(C) // (C // G))[None, :]).astype(f),
        "c_kmask": (np.arange(G * K2)[:, None] % K2 == np.arange(K2)[None, :]).astype(f),
    }


def kernel(**inputs):
    import numpy as _np
    import concourse.bacc as _bacc
    from concourse import mybir as _mybir
    from concourse.bass_utils import run_bass_kernel_spmd as _run

    nc = _bacc.Bacc("TRN2", target_bir_lowering=False, num_devices=1)
    arrays = {"x": _np.ascontiguousarray(inputs["x"])}
    for name in _INS:
        arrays[name] = _np.ascontiguousarray(inputs["L0_conv_" + name])
    for name in _INS1:
        arrays[name] = _np.ascontiguousarray(inputs["L1_conv_" + name])
    arrays["rpb_t"] = _np.ascontiguousarray(_np.asarray(inputs["L0_conv_rpb_table"]).T)
    arrays.update(constants())
    arrays = {"in_" + n: v for n, v in arrays.items()}
    aps = {n[3:]: nc.dram_tensor(n, v.shape, _mybir.dt.from_np(v.dtype), kind="ExternalInput").ap()
           for n, v in arrays.items()}
    out = nc.dram_tensor("out_0", arrays["in_x"].shape, _mybir.dt.float32, kind="ExternalOutput").ap()
    bass_window_block(nc, aps, out)
    r = _run(nc, [arrays], core_ids=[0])
    return r.results[0]["out_0"]
```
